# Optimizing a Trainium2 kernel written in Bass

```python
import numpy as np
import jax
import jax.numpy as jnp

def _softmax(x, axis=-1):
    return jax.nn.softmax(x, axis=axis)

def _gelu(x):
    return jax.nn.gelu(x, approximate=True)

def _silu(x):
    return jax.nn.silu(x)

def _sigmoid(x):
    return jax.nn.sigmoid(x)

def _layernorm(x, axis=-1, eps=1e-05):
    m = jnp.mean(x, axis=axis, keepdims=True)
    v = jnp.var(x, axis=axis, keepdims=True)
    return (x - m) / jnp.sqrt(v + eps)

def _scatter_add(tgt, idx, src, axis=0):
    return tgt.at[idx].add(src)

def _segment_sum(src, seg, n):
    return jax.ops.segment_sum(src, seg, n)
kernel_name = 'mk_adj_preln_d1_adj_r2_9495a3'

def setup_inputs(seed: int=0):
    np.random.seed(seed)
    _w = jnp.asarray

    def _rec_inputs():
        import jax
        import jax.numpy as jnp
        _gk = jax.random.key(seed)
        x = 7.22e-05 + 1 * jax.random.normal(jax.random.fold_in(_gk, 1), (8, 1024, 512), jnp.float32)
        _w = (1.0 + jnp.arange(1024, dtype=jnp.float32)) ** (-0.5)
        _w = _w / _w.mean()
        _pij = jnp.clip(0.00195312 * _w[:, None] * _w[None, :], 0.0, 1.0)
        _a = jax.random.uniform(jax.random.fold_in(_gk, 2), (8, 1024, 1024)) < _pij
        _a = jnp.logical_or(_a, jnp.eye(1024, dtype=bool))
        adj = _a.astype(jnp.int32)
        return (x, adj)
    x, adj = _rec_inputs()

    def _L0_gnn_setup():
        import jax, jax.numpy as jnp
        import numpy as np
        import math
        D_MODEL = 512
        N_HEADS = 16
        D_HEAD = D_MODEL // N_HEADS
        B, S = (4, 1024)
        key = jax.random.key(seed)
        ks = jax.random.split(key, 10)
        x = jax.random.normal(ks[0], (B, S, D_MODEL), dtype=jnp.float32)
        mask = jax.random.randint(ks[1], (B, S, S), 0, 2, dtype=jnp.int32)
        eye = jnp.eye(S, dtype=jnp.int32)[None]
        mask = jnp.maximum(mask, eye)
        std = 1.0 / math.sqrt(D_MODEL)
        Wq = jax.random.normal(ks[2], (D_MODEL, D_MODEL), dtype=jnp.float32) * std
        Wk = jax.random.normal(ks[3], (D_MODEL, D_MODEL), dtype=jnp.float32) * std
        Wv = jax.random.normal(ks[4], (D_MODEL, D_MODEL), dtype=jnp.float32) * std
        Wo = jax.random.normal(ks[5], (D_MODEL, D_MODEL), dtype=jnp.float32) * std
        bq = jnp.zeros((D_MODEL,), dtype=jnp.float32)
        bk = jnp.zeros((D_MODEL,), dtype=jnp.float32)
        bv = jnp.zeros((D_MODEL,), dtype=jnp.float32)
        bo = jnp.zeros((D_MODEL,), dtype=jnp.float32)
        return {'x': x, 'mask': mask, 'Wq': Wq, 'bq': bq, 'Wk': Wk, 'bk': bk, 'Wv': Wv, 'bv': bv, 'Wo': Wo, 'bo': bo}
    _L0_gnn_all = _L0_gnn_setup()
    _L0_gnn_in = {k: v for k, v in _L0_gnn_all.items() if k in ('Wq', 'bq', 'Wk', 'bk', 'Wv', 'bv', 'Wo', 'bo')}
    del _L0_gnn_all
    return {'x': x, 'adj': adj, 'L0_gnn_Wq': _L0_gnn_in['Wq'], 'L0_gnn_bq': _L0_gnn_in['bq'], 'L0_gnn_Wk': _L0_gnn_in['Wk'], 'L0_gnn_bk': _L0_gnn_in['bk'], 'L0_gnn_Wv': _L0_gnn_in['Wv'], 'L0_gnn_bv': _L0_gnn_in['bv'], 'L0_gnn_Wo': _L0_gnn_in['Wo'], 'L0_gnn_bo': _L0_gnn_in['bo']}

def reference(x, adj, L0_gnn_Wq, L0_gnn_bq, L0_gnn_Wk, L0_gnn_bk, L0_gnn_Wv, L0_gnn_bv, L0_gnn_Wo, L0_gnn_bo):
    import jax
    import jax.numpy as jnp

    def _L0_gnn_ref(x, mask, Wq, bq, Wk, bk, Wv, bv, Wo, bo):
        import jax, jax.numpy as jnp
        import numpy as np
        import math
        D_MODEL = 512
        N_HEADS = 16
        D_HEAD = D_MODEL // N_HEADS
        B, S = (4, 1024)
        b, s, _ = x.shape
        scale = 1.0 / math.sqrt(D_HEAD)

        def heads(t):
            return t.reshape(b, s, N_HEADS, D_HEAD).transpose(0, 2, 1, 3)
        q = heads(x @ Wq + bq)
        k = heads(x @ Wk + bk)
        v = heads(x @ Wv + bv)
        scores = jnp.einsum('bhqd,bhkd->bhqk', q, k) * scale
        scores = jnp.where(mask[:, None] == 0, -jnp.inf, scores)
        attn = jax.nn.softmax(scores, axis=-1)
        out = jnp.einsum('bhqk,bhkd->bhqd', attn, v)
        out = out.transpose(0, 2, 1, 3).reshape(b, s, D_MODEL)
        return out @ Wo + bo
    h = jnp.maximum(_layernorm(x, axis=-1), 0.0)
    x = x + _L0_gnn_ref(h, adj, L0_gnn_Wq, L0_gnn_bq, L0_gnn_Wk, L0_gnn_bk, L0_gnn_Wv, L0_gnn_bv, L0_gnn_Wo, L0_gnn_bo)
    return x

_drawn_inputs = setup_inputs


def setup_inputs(seed=0):
    import zlib

    import numpy as np

    out = dict(_drawn_inputs(seed))
    spreads = {'L0_gnn_bq': (0.0, 0.692),
     'L0_gnn_bk': (0.0, 0.8),
     'L0_gnn_bv': (0.0, 0.1),
     'L0_gnn_bo': (0.0, 0.1)}
    factors = {}
    for name, (base, spread) in spreads.items():
        noise = np.random.default_rng([zlib.crc32(name.encode()), seed]).standard_normal(out[name].shape)
        drawn = base * np.exp(spread * noise) if base else spread * noise
        out[name] = jnp.asarray(drawn.astype(out[name].dtype))
    for name, factor in factors.items():
        out[name] = (out[name] * factor).astype(out[name].dtype)
    return out
```

```python
import concourse.bass as bass
from concourse import mybir
from contextlib import ExitStack

B, S, D, H, P = 8, 1024, 512, 16, 128
DH = D // H
DC = D // P
QT = S // P
HG = P // DH
SCALE = float(DH) ** -0.5
EPS = 1e-5
MASKED = -1e30

F32 = mybir.dt.float32
I32 = mybir.dt.int32
ALU = mybir.AluOpType
ACT = mybir.ActivationFunctionType
AX = mybir.AxisListType


def general_attention(nc, always, flag, x, adj, Wq, bq, Wk, bk, Wv, bv, Wo, bo, ident, out, scratch):
    qT_s, kT_s, v_s, o_s = scratch
    ctx = ExitStack()
    with ctx:
        def sb(name, shape, dt=F32):
            return ctx.enter_context(nc.sbuf_tensor("g_" + name, shape, dt))

        def sem(name):
            return ctx.enter_context(nc.semaphore("g_" + name))

        w = [sb(n, [P, DC, D]) for n in ("wq", "wk", "wv", "wo")]
        bqk = [sb(n, [P, DC]) for n in ("bq", "bk")]
        bv_row, bo_row = sb("bv_row", [P, D]), sb("bo_row", [P, D])
        idt = sb("ident", [P, P])
        x_in = sb("x_in", [P, D])
        stats, mv = sb("stats", [P, 6]), sb("mv", [P, 2])
        lnv, rstd = sb("lnv", [P, 1]), sb("rstd", [P, 1])
        eps = sb("eps", [P, 1])
        xn = sb("xn", [P, D])
        hT = sb("hT", [P, DC, P])
        qkT = [sb(n, [P, DC, P]) for n in ("qT", "kT")]
        v_out = sb("v_out", [P, D])
        edges = sb("edges", [P, QT, S], I32)
        bias = sb("bias", [P, QT, S])
        qT, kT = sb("qT_h", [DH, S]), sb("kT_h", [DH, S])
        v = sb("v_h", [P, QT, DH])
        masked = sb("masked", [P, S])
        rowmax, shift = sb("rowmax", [P, 1]), sb("shift", [P, 1])
        prob = sb("prob", [P, S])
        rowsum, rinv = sb("rowsum", [P, 1]), sb("rinv", [P, 1])
        probT = sb("probT", [P, QT, P])
        o_h = sb("o_h", [P, QT, DH])
        o_in, oT = sb("o_in", [P, D]), sb("oT", [P, DC, P])
        y, y_out = sb("y", [P, D]), sb("y_out", [P, D])

        ps = ctx.enter_context(nc.psum_tensor("g_ps", [P, 8, 512], F32))
        ps_t = ps[:, 0, :].rearrange("p (c n) -> p c n", c=DC)
        ps_q = [ps[:, 1 + j, :].rearrange("p (c n) -> p c n", c=DC) for j in range(2)]
        ps_v = ps[:, 3, :]
        ps_s = ps[:, 4:6, :].rearrange("p a n -> p (a n)")
        ps_pt = ps[:, 6:8, :].rearrange("p a (k n) -> p (a k) n", n=P)
        ps_o = ps[:, 2, 0:DH]
        ps_y = ps[:, 1, :]

        masked_ready = sem("masked_ready")
        gap = sb("gap", [P, 1])
        loaded, eps_set = sem("loaded"), sem("eps_set")
        x_loaded, mv_ready, stats_ready, ln_ready, rstd_ready, xn_ready, xT_ready, hT_ready, proj_ready, proj_copied, qkv_stored = (
            sem(n) for n in ("x_loaded", "mv_ready", "stats_ready", "ln_ready", "rstd_ready", "xn_ready", "xT_ready", "hT_ready",
                             "proj_ready", "proj_copied", "qkv_stored"))
        edges_loaded, bias_ready, head_loaded = sem("edges_loaded"), sem("bias_ready"), sem("head_loaded")
        score_ready, max_ready, shift_ready, prob_ready, probT_ready, probT_copied, o_ready, rinv_ready, o_copied, o_stored = (
            sem(n) for n in ("score_ready", "max_ready", "shift_ready", "prob_ready", "probT_ready", "probT_copied", "o_ready",
                             "rinv_ready", "o_copied", "o_stored"))
        o_loaded, oT_ready, oT_copied, y_ready, y_biased, y_done, y_stored = (
            sem(n) for n in ("o_loaded", "oT_ready", "oT_copied", "y_ready", "y_biased", "y_done", "y_stored"))

        WEIGHTS = 16 * 9
        TOKT = B * QT
        x_t = x.rearrange("b (t p) d -> (b t) p d", p=P)
        out_t = out.rearrange("b (t p) d -> (b t) p d", p=P)
        v_t = v_s.rearrange("b (t p) d -> (b t) p d", p=P)
        o_t = o_s.rearrange("b (t p) d -> (b t) p d", p=P)
        qk_t = [s.rearrange("b (c p) (t n) -> b t p c n", p=P, n=P) for s in (qT_s, kT_s)]

        block = ctx.enter_context(nc.Block())

        def gated(eng, program):
            if always:
                program()
                return
            wanted = eng.value_load(flag, min_val=0, max_val=1)
            with eng.If(wanted > 0):
                program()

        @block.sync
        def _(sp):
            def program():
                for n, wt in enumerate((Wq, Wk, Wv, Wo)):
                    sp.dma_start(w[n][:], wt.rearrange("(c p) n -> p c n", p=P)).then_inc(loaded, 16)
                for n, bias_ in enumerate((bq, bk)):
                    sp.dma_start(bqk[n][:], bias_).then_inc(loaded, 16)
                sp.dma_start(bv_row[:], bv.partition_broadcast(P)).then_inc(loaded, 16)
                sp.dma_start(bo_row[:], bo.partition_broadcast(P)).then_inc(loaded, 16)
                sp.dma_start(idt[:], ident).then_inc(loaded, 16)
                with sp.Fori(0, B) as b:
                    for t in range(QT):
                        i = b * QT + t
                        sp.dma_start(x_in[:], x_t[bass.ds(i, 1)].rearrange("a p d -> p (a d)")).then_inc(x_loaded, 16)
                        sp.wait_ge(proj_copied, 3 * i + 3)
                        for n in range(2):
                            sp.dma_start(qk_t[n][bass.ds(b, 1), t].rearrange("a p c n -> p (a c) n"), qkT[n][:]).then_inc(qkv_stored, 16)
                        sp.dma_start(v_t[bass.ds(i, 1)].rearrange("a p d -> p (a d)"), v_out[:]).then_inc(qkv_stored, 16)
                sp.wait_ge(qkv_stored, 48 * TOKT)
                with sp.Fori(0, B) as b:
                    sp.dma_start(edges[:], adj[bass.ds(b, 1)].rearrange("a (t p) k -> p (a t) k", p=P)).then_inc(edges_loaded, 16)
                    with sp.Fori(0, H) as h:
                        u = b * H + h
                        sp.dma_start(qT[:], qT_s[bass.ds(b, 1), bass.ds(h * DH, DH)].rearrange("a p n -> p (a n)")).then_inc(head_loaded, 16)
                        sp.dma_start(kT[:], kT_s[bass.ds(b, 1), bass.ds(h * DH, DH)].rearrange("a p n -> p (a n)")).then_inc(head_loaded, 16)
                        sp.dma_start(v[:], v_s[bass.ds(b, 1), :, bass.ds(h * DH, DH)].rearrange("a (t p) n -> p (a t) n", p=P)).then_inc(head_loaded, 16)
                        sp.wait_ge(o_copied, QT * u + QT)
                        sp.dma_start(o_s[bass.ds(b, 1), :, bass.ds(h * DH, DH)].rearrange("a (t p) n -> p (a t) n", p=P), o_h[:]).then_inc(o_stored, 16)
                sp.wait_ge(o_stored, 16 * B * H)
                with sp.Fori(0, TOKT) as i:
                    sp.dma_start(o_in[:], o_t[bass.ds(i, 1)].rearrange("a p d -> p (a d)")).then_inc(o_loaded, 16)
                    sp.dma_start(x_in[:], x_t[bass.ds(i, 1)].rearrange("a p d -> p (a d)")).then_inc(o_loaded, 16)
                    sp.wait_ge(y_done, i + 1)
                    sp.dma_start(out_t[bass.ds(i, 1)].rearrange("a p d -> p (a d)"), y_out[:]).then_inc(y_stored, 16)
                sp.wait_ge(y_stored, 16 * TOKT)
            gated(sp, program)

        @block.vector
        def _(dve):
            def program():
                nc.vector.memset(eps[:], EPS).then_inc(eps_set, 1)
                dve.wait_ge(loaded, WEIGHTS)
                with dve.Fori(0, TOKT) as i:
                    dve.wait_ge(x_loaded, 16 * i + 16)
                    nc.vector.bn_stats(stats[:], x_in[:]).then_inc(stats_ready, 1)
                    dve.wait_ge(stats_ready, i + 1)
                    nc.vector.memset(gap[:], 0.0)
                    nc.vector.bn_aggr(mv[:], stats[:]).then_inc(mv_ready, 1)
                    dve.wait_ge(rstd_ready, i + 1)
                    nc.vector.tensor_scalar(xn[:], x_in[:], mv[:, 0:1], rstd[:], ALU.subtract, ALU.mult).then_inc(xn_ready, 1)
                    dve.wait_ge(proj_ready, i + 1)
                    for n in range(2):
                        for m in range(DC):
                            last = nc.vector.tensor_scalar(qkT[n][:, m, :], ps_q[n][:, m, :], bqk[n][:, m:m + 1], None, ALU.add)
                        last.then_inc(proj_copied, 1)
                    nc.vector.tensor_tensor(v_out[:], ps_v, bv_row[:], ALU.add).then_inc(proj_copied, 1)
                    dve.wait_ge(qkv_stored, 48 * i + 48)
                with dve.Fori(0, B) as b:
                    dve.wait_ge(edges_loaded, 16 * b + 16)
                    nc.vector.tensor_scalar(bias[:], edges[:], 0.0, MASKED, ALU.is_equal, ALU.mult).then_inc(bias_ready, 1)
                    dve.wait_ge(bias_ready, b + 1)
                    nc.vector.memset(gap[:], 0.0)
                    with dve.Fori(0, H) as h:
                        for t in range(QT):
                            n = (b * H + h) * QT + t
                            dve.wait_ge(score_ready, n + 1)
                            nc.vector.tensor_tensor(masked[:], ps_s, bias[:, t, :], ALU.add).then_inc(masked_ready, 1)
                            dve.wait_ge(masked_ready, n + 1)
                            nc.vector.reduce_max(rowmax[:], masked[:], AX.X).then_inc(max_ready, 1)
                            dve.wait_ge(max_ready, n + 1)
                            nc.vector.tensor_scalar(shift[:], rowmax[:], -SCALE, None, ALU.mult).then_inc(shift_ready, 1)
                            dve.wait_ge(probT_ready, n + 1)
                            nc.vector.tensor_copy(probT[:], ps_pt).then_inc(probT_copied, 1)
                            nc.vector.reciprocal(rinv[:], rowsum[:]).then_inc(rinv_ready, 1)
                            dve.wait_ge(rinv_ready, n + 1)
                            dve.wait_ge(o_ready, n + 1)
                            nc.vector.tensor_scalar(o_h[:, t, :], ps_o, rinv[:], None, ALU.mult).then_inc(o_copied, 1)
                        dve.wait_ge(o_stored, 16 * (b * H + h) + 16)
                with dve.Fori(0, TOKT) as i:
                    dve.wait_ge(o_loaded, 32 * i + 32)
                    dve.wait_ge(oT_ready, i + 1)
                    nc.vector.tensor_copy(oT[:], ps_t).then_inc(oT_copied, 1)
                    dve.wait_ge(y_ready, i + 1)
                    nc.vector.tensor_tensor(y[:], ps_y, bo_row[:], ALU.add).then_inc(y_biased, 1)
                    dve.wait_ge(y_biased, i + 1)
                    nc.vector.tensor_tensor(y_out[:], y[:], x_in[:], ALU.add).then_inc(y_done, 1)
                    dve.wait_ge(y_stored, 16 * i + 16)
            gated(dve, program)

        @block.scalar
        def _(act):
            def program():
                act.wait_ge(eps_set, 1)
                with act.Fori(0, TOKT) as i:
                    act.wait_ge(mv_ready, i + 1)
                    nc.scalar.activation(lnv[:], mv[:, 1:2], ACT.Ln, bias=eps[:]).then_inc(ln_ready, 1)
                    act.wait_ge(ln_ready, i + 1)
                    nc.scalar.activation(rstd[:], lnv[:], ACT.Exp, scale=-0.5).then_inc(rstd_ready, 1)
                    act.wait_ge(xT_ready, i + 1)
                    nc.scalar.activation(hT[:], ps_t, ACT.Relu).then_inc(hT_ready, 1)
                with act.Fori(0, B * H) as u:
                    for t in range(QT):
                        n = u * QT + t
                        act.wait_ge(shift_ready, n + 1)
                        nc.scalar.activation(prob[:], masked[:], ACT.Exp, bias=shift[:], scale=SCALE, accum_out=rowsum[:]).then_inc(prob_ready, 1)
            gated(act, program)

        @block.tensor
        def _(pe):
            def program():
                pe.wait_ge(loaded, WEIGHTS)
                with pe.Fori(0, TOKT) as i:
                    pe.wait_ge(xn_ready, i + 1)
                    for c in range(DC):
                        last = nc.tensor.transpose(ps_t[:, c, :], xn[:, c * P:(c + 1) * P], idt[:])
                    last.then_inc(xT_ready, 1)
                    pe.wait_ge(hT_ready, i + 1)
                    for n in range(2):
                        for m in range(DC):
                            for c in range(DC):
                                nc.tensor.matmul(ps_q[n][:, m, :], w[n][:, c, m * P:(m + 1) * P], hT[:, c, :], start=c == 0, stop=c == DC - 1)
                    for c in range(DC):
                        last = nc.tensor.matmul(ps_v, hT[:, c, :], w[2][:, c, :], start=c == 0, stop=c == DC - 1)
                    last.then_inc(proj_ready, 1)
                with pe.Fori(0, B * H) as u:
                    pe.wait_ge(head_loaded, 48 * u + 48)
                    for t in range(QT):
                        n = u * QT + t
                        for half in range(2):
                            last = nc.tensor.matmul(ps[:, 4 + half, :], qT[:, t * P:(t + 1) * P], kT[:, half * 512:(half + 1) * 512], start=True, stop=True)
                        last.then_inc(score_ready, 1)
                        pe.wait_ge(prob_ready, n + 1)
                        for k in range(QT):
                            last = nc.tensor.transpose(ps_pt[:, k, :], prob[:, k * P:(k + 1) * P], idt[:])
                        last.then_inc(probT_ready, 1)
                        pe.wait_ge(probT_copied, n + 1)
                        for k in range(QT):
                            last = nc.tensor.matmul(ps_o, probT[:, k, :], v[:, k, :], start=k == 0, stop=k == QT - 1)
                        last.then_inc(o_ready, 1)
                with pe.Fori(0, TOKT) as i:
                    pe.wait_ge(o_loaded, 32 * i + 32)
                    for c in range(DC):
                        last = nc.tensor.transpose(ps_t[:, c, :], o_in[:, c * P:(c + 1) * P], idt[:])
                    last.then_inc(oT_ready, 1)
                    pe.wait_ge(oT_copied, i + 1)
                    for c in range(DC):
                        last = nc.tensor.matmul(ps_y, oT[:, c, :], w[3][:, c, :], start=c == 0, stop=c == DC - 1)
                    last.then_inc(y_ready, 1)
            gated(pe, program)


def program(nc, x, adj, Wq, bq, Wk, bk, Wv, bv, Wo, bo, ident, out):
    scratch = [nc.dram_tensor(n, s, F32, kind="Internal").ap()
               for n, s in (("qT_s", [B, D, S]), ("kT_s", [B, D, S]), ("v_s", [B, S, D]), ("o_s", [B, S, D]))]
    general_attention(nc, True, None, x, adj, Wq, bq, Wk, bk, Wv, bv, Wo, bo, ident, out, scratch)


def kernel(x, adj, L0_gnn_Wq, L0_gnn_bq, L0_gnn_Wk, L0_gnn_bk, L0_gnn_Wv, L0_gnn_bv, L0_gnn_Wo, L0_gnn_bo):
    import numpy as np
    import concourse.bacc as bacc
    from concourse.bass_utils import run_bass_kernel_spmd

    nc = bacc.Bacc("TRN2", target_bir_lowering=False, num_devices=1)
    arrays = {
        "x": np.ascontiguousarray(x), "adj": np.ascontiguousarray(adj),
        "Wq": L0_gnn_Wq, "bq": np.asarray(L0_gnn_bq).reshape(DC, P).T, "Wk": L0_gnn_Wk, "bk": np.asarray(L0_gnn_bk).reshape(DC, P).T,
        "Wv": L0_gnn_Wv, "bv": L0_gnn_bv, "Wo": L0_gnn_Wo, "bo": L0_gnn_bo,
        "ident": np.eye(P, dtype=np.float32),
    }
    arrays = {n: np.ascontiguousarray(a) for n, a in arrays.items()}
    args = [nc.dram_tensor(n, a.shape, mybir.dt.from_np(a.dtype), kind="ExternalInput").ap() for n, a in arrays.items()]
    out = nc.dram_tensor("out", (B, S, D), F32, kind="ExternalOutput").ap()
    program(nc, *args, out)
    r = run_bass_kernel_spmd(nc, [arrays], core_ids=[0])
    return r.results[0]["out"]
```

```python
import concourse.bass as bass
from concourse import mybir
from contextlib import ExitStack

B, S, D, H, P = 8, 1024, 512, 16, 128
DH = D // H
DC = D // P
QT = S // P
HG = P // DH
SCALE = float(DH) ** -0.5
EPS = 1e-5
MASKED = -1e30

F32 = mybir.dt.float32
I32 = mybir.dt.int32
ALU = mybir.AluOpType
ACT = mybir.ActivationFunctionType
AX = mybir.AxisListType


def general_attention(nc, flag, x, adj, Wq, bq, Wk, bk, Wv, bv, Wo, bo, ident, out, scratch):
    qT_s, kT_s, v_s, o_s = scratch
    ctx = ExitStack()
    with ctx:
        def sb(name, shape, dt=F32):
            return ctx.enter_context(nc.sbuf_tensor("g_" + name, shape, dt))

        def sem(name):
            return ctx.enter_context(nc.semaphore("g_" + name))

        w = [sb(n, [P, DC, D]) for n in ("wq", "wk", "wv", "wo")]
        bqk = [sb(n, [P, DC]) for n in ("bq", "bk")]
        bv_row, bo_row = sb("bv_row", [P, D]), sb("bo_row", [P, D])
        idt = sb("ident", [P, P])
        x_in = sb("x_in", [P, D])
        stats, mv = sb("stats", [P, 6]), sb("mv", [P, 2])
        lnv, rstd = sb("lnv", [P, 1]), sb("rstd", [P, 1])
        eps = sb("eps", [P, 1])
        xn = sb("xn", [P, D])
        hT = sb("hT", [P, DC, P])
        qkT = [sb(n, [P, DC, P]) for n in ("qT", "kT")]
        v_out = sb("v_out", [P, D])
        edges = sb("edges", [P, QT, S], I32)
        bias = sb("bias", [P, QT, S])
        qT, kT = sb("qT_h", [DH, S]), sb("kT_h", [DH, S])
        v = sb("v_h", [P, QT, DH])
        masked = sb("masked", [P, S])
        rowmax, shift = sb("rowmax", [P, 1]), sb("shift", [P, 1])
        prob = sb("prob", [P, S])
        rowsum, rinv = sb("rowsum", [P, 1]), sb("rinv", [P, 1])
        probT = sb("probT", [P, QT, P])
        o_h = sb("o_h", [P, QT, DH])
        o_in, oT = sb("o_in", [P, D]), sb("oT", [P, DC, P])
        y, y_out = sb("y", [P, D]), sb("y_out", [P, D])

        ps = ctx.enter_context(nc.psum_tensor("g_ps", [P, 8, 512], F32))
        ps_t = ps[:, 0, :].rearrange("p (c n) -> p c n", c=DC)
        ps_q = [ps[:, 1 + j, :].rearrange("p (c n) -> p c n", c=DC) for j in range(2)]
        ps_v = ps[:, 3, :]
        ps_s = ps[:, 4:6, :].rearrange("p a n -> p (a n)")
        ps_pt = ps[:, 6:8, :].rearrange("p a (k n) -> p (a k) n", n=P)
        ps_o = ps[:, 2, 0:DH]
        ps_y = ps[:, 1, :]

        masked_ready = sem("masked_ready")
        gap = sb("gap", [P, 1])
        loaded, eps_set = sem("loaded"), sem("eps_set")
        x_loaded, mv_ready, stats_ready, ln_ready, rstd_ready, xn_ready, xT_ready, hT_ready, proj_ready, proj_copied, qkv_stored = (
            sem(n) for n in ("x_loaded", "mv_ready", "stats_ready", "ln_ready", "rstd_ready", "xn_ready", "xT_ready", "hT_ready",
                             "proj_ready", "proj_copied", "qkv_stored"))
        edges_loaded, bias_ready, head_loaded = sem("edges_loaded"), sem("bias_ready"), sem("head_loaded")
        score_ready, max_ready, shift_ready, prob_ready, probT_ready, probT_copied, o_ready, rinv_ready, o_copied, o_stored = (
            sem(n) for n in ("score_ready", "max_ready", "shift_ready", "prob_ready", "probT_ready", "probT_copied", "o_ready",
                             "rinv_ready", "o_copied", "o_stored"))
        o_loaded, oT_ready, oT_copied, y_ready, y_biased, y_done, y_stored = (
            sem(n) for n in ("o_loaded", "oT_ready", "oT_copied", "y_ready", "y_biased", "y_done", "y_stored"))

        WEIGHTS = 16 * 9
        TOKT = B * QT
        x_t = x.rearrange("b (t p) d -> (b t) p d", p=P)
        out_t = out.rearrange("b (t p) d -> (b t) p d", p=P)
        v_t = v_s.rearrange("b (t p) d -> (b t) p d", p=P)
        o_t = o_s.rearrange("b (t p) d -> (b t) p d", p=P)
        qk_t = [s.rearrange("b (c p) (t n) -> b t p c n", p=P, n=P) for s in (qT_s, kT_s)]

        block = ctx.enter_context(nc.Block())

        def gated(eng, program):
            wanted = eng.value_load(flag, min_val=0, max_val=1)
            with eng.If(wanted > 0):
                program()

        @block.sync
        def _(sp):
            def program():
                for n, wt in enumerate((Wq, Wk, Wv, Wo)):
                    sp.dma_start(w[n][:], wt.rearrange("(c p) n -> p c n", p=P)).then_inc(loaded, 16)
                for n, bias_ in enumerate((bq, bk)):
                    sp.dma_start(bqk[n][:], bias_).then_inc(loaded, 16)
                sp.dma_start(bv_row[:], bv.partition_broadcast(P)).then_inc(loaded, 16)
                sp.dma_start(bo_row[:], bo.partition_broadcast(P)).then_inc(loaded, 16)
                sp.dma_start(idt[:], ident).then_inc(loaded, 16)
                with sp.Fori(0, B) as b:
                    for t in range(QT):
                        i = b * QT + t
                        sp.dma_start(x_in[:], x_t[bass.ds(i, 1)].rearrange("a p d -> p (a d)")).then_inc(x_loaded, 16)
                        sp.wait_ge(proj_copied, 3 * i + 3)
                        for n in range(2):
                            sp.dma_start(qk_t[n][bass.ds(b, 1), t].rearrange("a p c n -> p (a c) n"), qkT[n][:]).then_inc(qkv_stored, 16)
                        sp.dma_start(v_t[bass.ds(i, 1)].rearrange("a p d -> p (a d)"), v_out[:]).then_inc(qkv_stored, 16)
                sp.wait_ge(qkv_stored, 48 * TOKT)
                with sp.Fori(0, B) as b:
                    sp.dma_start(edges[:], adj[bass.ds(b, 1)].rearrange("a (t p) k -> p (a t) k", p=P)).then_inc(edges_loaded, 16)
                    with sp.Fori(0, H) as h:
                        u = b * H + h
                        sp.dma_start(qT[:], qT_s[bass.ds(b, 1), bass.ds(h * DH, DH)].rearrange("a p n -> p (a n)")).then_inc(head_loaded, 16)
                        sp.dma_start(kT[:], kT_s[bass.ds(b, 1), bass.ds(h * DH, DH)].rearrange("a p n -> p (a n)")).then_inc(head_loaded, 16)
                        sp.dma_start(v[:], v_s[bass.ds(b, 1), :, bass.ds(h * DH, DH)].rearrange("a (t p) n -> p (a t) n", p=P)).then_inc(head_loaded, 16)
                        sp.wait_ge(o_copied, QT * u + QT)
                        sp.dma_start(o_s[bass.ds(b, 1), :, bass.ds(h * DH, DH)].rearrange("a (t p) n -> p (a t) n", p=P), o_h[:]).then_inc(o_stored, 16)
                sp.wait_ge(o_stored, 16 * B * H)
                with sp.Fori(0, TOKT) as i:
                    sp.dma_start(o_in[:], o_t[bass.ds(i, 1)].rearrange("a p d -> p (a d)")).then_inc(o_loaded, 16)
                    sp.dma_start(x_in[:], x_t[bass.ds(i, 1)].rearrange("a p d -> p (a d)")).then_inc(o_loaded, 16)
                    sp.wait_ge(y_done, i + 1)
                    sp.dma_start(out_t[bass.ds(i, 1)].rearrange("a p d -> p (a d)"), y_out[:]).then_inc(y_stored, 16)
                sp.wait_ge(y_stored, 16 * TOKT)
            gated(sp, program)

        @block.vector
        def _(dve):
            def program():
                nc.vector.memset(eps[:], EPS).then_inc(eps_set, 1)
                dve.wait_ge(loaded, WEIGHTS)
                with dve.Fori(0, TOKT) as i:
                    dve.wait_ge(x_loaded, 16 * i + 16)
                    nc.vector.bn_stats(stats[:], x_in[:]).then_inc(stats_ready, 1)
                    dve.wait_ge(stats_ready, i + 1)
                    nc.vector.memset(gap[:], 0.0)
                    nc.vector.bn_aggr(mv[:], stats[:]).then_inc(mv_ready, 1)
                    dve.wait_ge(rstd_ready, i + 1)
                    nc.vector.tensor_scalar(xn[:], x_in[:], mv[:, 0:1], rstd[:], ALU.subtract, ALU.mult).then_inc(xn_ready, 1)
                    dve.wait_ge(proj_ready, i + 1)
                    for n in range(2):
                        for m in range(DC):
                            last = nc.vector.tensor_scalar(qkT[n][:, m, :], ps_q[n][:, m, :], bqk[n][:, m:m + 1], None, ALU.add)
                        last.then_inc(proj_copied, 1)
                    nc.vector.tensor_tensor(v_out[:], ps_v, bv_row[:], ALU.add).then_inc(proj_copied, 1)
                    dve.wait_ge(qkv_stored, 48 * i + 48)
                with dve.Fori(0, B) as b:
                    dve.wait_ge(edges_loaded, 16 * b + 16)
                    nc.vector.tensor_scalar(bias[:], edges[:], 0.0, MASKED, ALU.is_equal, ALU.mult).then_inc(bias_ready, 1)
                    dve.wait_ge(bias_ready, b + 1)
                    nc.vector.memset(gap[:], 0.0)
                    with dve.Fori(0, H) as h:
                        for t in range(QT):
                            n = (b * H + h) * QT + t
                            dve.wait_ge(score_ready, n + 1)
                            nc.vector.tensor_tensor(masked[:], ps_s, bias[:, t, :], ALU.add).then_inc(masked_ready, 1)
                            dve.wait_ge(masked_ready, n + 1)
                            nc.vector.reduce_max(rowmax[:], masked[:], AX.X).then_inc(max_ready, 1)
                            dve.wait_ge(max_ready, n + 1)
                            nc.vector.tensor_scalar(shift[:], rowmax[:], -SCALE, None, ALU.mult).then_inc(shift_ready, 1)
                            dve.wait_ge(probT_ready, n + 1)
                            nc.vector.tensor_copy(probT[:], ps_pt).then_inc(probT_copied, 1)
                            nc.vector.reciprocal(rinv[:], rowsum[:]).then_inc(rinv_ready, 1)
                            dve.wait_ge(rinv_ready, n + 1)
                            dve.wait_ge(o_ready, n + 1)
                            nc.vector.tensor_scalar(o_h[:, t, :], ps_o, rinv[:], None, ALU.mult).then_inc(o_copied, 1)
                        dve.wait_ge(o_stored, 16 * (b * H + h) + 16)
                with dve.Fori(0, TOKT) as i:
                    dve.wait_ge(o_loaded, 32 * i + 32)
                    dve.wait_ge(oT_ready, i + 1)
                    nc.vector.tensor_copy(oT[:], ps_t).then_inc(oT_copied, 1)
                    dve.wait_ge(y_ready, i + 1)
                    nc.vector.tensor_tensor(y[:], ps_y, bo_row[:], ALU.add).then_inc(y_biased, 1)
                    dve.wait_ge(y_biased, i + 1)
                    nc.vector.tensor_tensor(y_out[:], y[:], x_in[:], ALU.add).then_inc(y_done, 1)
                    dve.wait_ge(y_stored, 16 * i + 16)
            gated(dve, program)

        @block.scalar
        def _(act):
            def program():
                act.wait_ge(eps_set, 1)
                with act.Fori(0, TOKT) as i:
                    act.wait_ge(mv_ready, i + 1)
                    nc.scalar.activation(lnv[:], mv[:, 1:2], ACT.Ln, bias=eps[:]).then_inc(ln_ready, 1)
                    act.wait_ge(ln_ready, i + 1)
                    nc.scalar.activation(rstd[:], lnv[:], ACT.Exp, scale=-0.5).then_inc(rstd_ready, 1)
                    act.wait_ge(xT_ready, i + 1)
                    nc.scalar.activation(hT[:], ps_t, ACT.Relu).then_inc(hT_ready, 1)
                with act.Fori(0, B * H) as u:
                    for t in range(QT):
                        n = u * QT + t
                        act.wait_ge(shift_ready, n + 1)
                        nc.scalar.activation(prob[:], masked[:], ACT.Exp, bias=shift[:], scale=SCALE, accum_out=rowsum[:]).then_inc(prob_ready, 1)
            gated(act, program)

        @block.tensor
        def _(pe):
            def program():
                pe.wait_ge(loaded, WEIGHTS)
                with pe.Fori(0, TOKT) as i:
                    pe.wait_ge(xn_ready, i + 1)
                    for c in range(DC):
                        last = nc.tensor.transpose(ps_t[:, c, :], xn[:, c * P:(c + 1) * P], idt[:])
                    last.then_inc(xT_ready, 1)
                    pe.wait_ge(hT_ready, i + 1)
                    for n in range(2):
                        for m in range(DC):
                            for c in range(DC):
                                nc.tensor.matmul(ps_q[n][:, m, :], w[n][:, c, m * P:(m + 1) * P], hT[:, c, :], start=c == 0, stop=c == DC - 1)
                    for c in range(DC):
                        last = nc.tensor.matmul(ps_v, hT[:, c, :], w[2][:, c, :], start=c == 0, stop=c == DC - 1)
                    last.then_inc(proj_ready, 1)
                with pe.Fori(0, B * H) as u:
                    pe.wait_ge(head_loaded, 48 * u + 48)
                    for t in range(QT):
                        n = u * QT + t
                        for half in range(2):
                            last = nc.tensor.matmul(ps[:, 4 + half, :], qT[:, t * P:(t + 1) * P], kT[:, half * 512:(half + 1) * 512], start=True, stop=True)
                        last.then_inc(score_ready, 1)
                        pe.wait_ge(prob_ready, n + 1)
                        for k in range(QT):
                            last = nc.tensor.transpose(ps_pt[:, k, :], prob[:, k * P:(k + 1) * P], idt[:])
                        last.then_inc(probT_ready, 1)
                        pe.wait_ge(probT_copied, n + 1)
                        for k in range(QT):
                            last = nc.tensor.matmul(ps_o, probT[:, k, :], v[:, k, :], start=k == 0, stop=k == QT - 1)
                        last.then_inc(o_ready, 1)
                with pe.Fori(0, TOKT) as i:
                    pe.wait_ge(o_loaded, 32 * i + 32)
                    for c in range(DC):
                        last = nc.tensor.transpose(ps_t[:, c, :], o_in[:, c * P:(c + 1) * P], idt[:])
                    last.then_inc(oT_ready, 1)
                    pe.wait_ge(oT_copied, i + 1)
                    for c in range(DC):
                        last = nc.tensor.matmul(ps_y, oT[:, c, :], w[3][:, c, :], start=c == 0, stop=c == DC - 1)
                    last.then_inc(y_ready, 1)
            gated(pe, program)


F16 = mybir.dt.float16
BF16 = mybir.dt.bfloat16
HALF = 512
UNITS = D // P
STEPS = QT
TILES = STEPS * HG
UP = 64.0
RING = 2 * HG
W_MAX = 120.0 / UP
LIM_W, LIM_B, LIM_N, LIM_QK = 0, 4, 5, 5 + 2 * HG
LIMITS = LIM_QK + HG
RMAX = bass.bass_isa.ReduceOp.max
BOUND_SQ = 36.0 ** 2 * 0.96

PROJ = [("q", 0), ("q", 1), ("k", 0), ("k", 1)]


def chunk_slots(up, first, last):
    if up == 0:
        ys = [] if first else [("y", t) for t in range(QT)]
        at = list(enumerate(PROJ + [("v", 0)])) + [(5 + n, y) for n, y in enumerate(ys)] + [(13, ("v", 1)), (14, ("n", 0))]
    elif up < UNITS - 1:
        at = [(2 * n + 1, c) for n, c in enumerate(PROJ + [("v", 0), ("v", 1), ("n", 0)])]
    elif last:
        at = []
    else:
        at = [(n, ("t", n)) for n in range(QT)] + [(8 + n, c) for n, c in enumerate(PROJ + [("v", 0), ("v", 1), ("n", 0)])]
    return dict(at)


def chunk_list(up, first, last):
    return [c for _, c in sorted(chunk_slots(up, first, last).items())]


PRO_CHUNKS = [("t", n) for n in range(QT)] + PROJ + [("v", 0), ("v", 1), ("n", 0)]
ALL = "qkvtyn"
SPLIT = "qkt"


def count(kinds, chunks):
    return sum(c[0] in kinds for c in chunks)


def chunks_before(kinds, b, up, first):
    n = count(kinds, PRO_CHUNKS)
    here = sum(count(kinds, chunk_list(k, first, False)) for k in range(up))
    if first:
        return n + here
    zero = sum(count(kinds, chunk_list(k, True, False)) for k in range(UNITS))
    each = sum(count(kinds, chunk_list(k, False, False)) for k in range(UNITS))
    return (b * each + (n + zero - each)) + here


def fast_attention(nc, x, adjT, Wq, bq, Wk, bk, Wv, bv, Wo, bo, ident, headones, rowones, out, flag):
    ctx = ExitStack()
    with ctx:
        def sb(name, shape, dt=F32):
            return ctx.enter_context(nc.sbuf_tensor(name, shape, dt))

        def sem(name):
            return ctx.enter_context(nc.semaphore(name))

        w_hi = [sb(f"w{n}_hi", [P, DC, D], F16) for n in "qkvo"]
        w_lo = [sb(f"w{n}_lo", [P, DC, D], F16) for n in "qkvo"]
        WQ, WK, WV, WO = range(4)
        b_in = sb("b_in", [P, 3, DC])
        b_up = sb("b_up", [P, 3, DC])
        bo_row = sb("bo_row", [P, D])
        idt = sb("idt", [P, P])
        head1 = sb("head1", [P, HG], BF16)
        ones = sb("ones", [P, 2, DH])
        eps = sb("eps", [P, 1])
        gap = sb("gap", [P, 1])
        limits = sb("limits", [P, LIMITS])
        largest = sb("largest", [P, 1])
        mask = sb("mask", [P, QT, S], BF16)
        edges = sb("edges", [P, S], I32)
        hT_hi, hT_lo = sb("hT_hi", [P, DC, S], F16), sb("hT_lo", [P, DC, S], F16)
        oT_hi, oT_lo = sb("oT_hi", [P, DC, S], F16), sb("oT_lo", [P, DC, S], F16)
        x_in = sb("x_in", [P, 2, D])
        stats, mv = sb("stats", [P, QT, 6]), sb("mv", [P, QT, 2])
        rstd = sb("rstd", [P, QT])
        y_out = sb("y_out", [P, 2, D])
        part = {c: sb(f"{c}_part", [P, 2, S], F16) for c in "qk"}
        squares = sb("squares", [P, 2, S], BF16)
        norms = sb("norms", [P, 2 * QT * HG])
        stack = {c: sb(f"{c}_stack", [P, 2, HG, S], F16) for c in "qk"}
        v_sb = sb("v_sb", [P, 2, QT, P])
        ring = sb("ring", [P, RING, S])
        acc = sb("acc", [P, HG, S])
        o_raw = sb("o_raw", [P, S])
        rden = sb("rden", [P, HALF])
        rden_all = sb("rden_all", [P, S])

        ps = ctx.enter_context(nc.psum_tensor("ps", [P, 8, HALF], F32))
        BANK_O, BANK_D, BANK_M = 4, 6, 7
        ps_o = ps[:, BANK_O:BANK_O + 2, :].rearrange("p a n -> p (a n)")
        misc = ps[:, BANK_M, :]

        def ps_s(j):
            return ps[:, 2 * (j % 2):2 * (j % 2) + 2, :].rearrange("p a n -> p (a n)")

        names = ("w_loaded_0 w_loaded_1 w_hi_ready w_lo_ready const_ready const_loaded x_loaded_0 x_loaded_1 edges_loaded stack_loaded stored_0 stored_1 "
                 "chunk_ready chunk_act chunk_free score_ready score_masked prob_ready pv_done sum_done den_done "
                 "o_copied ln_done rden_ready o_scaled o_hi_ready o_ready shuffled mask_ready x_stats x_stat_each x_mean ln_var rstd_ready "
                 "x_normed x_biased y_ready limits_ready limits_everywhere verdict_step")
        s = {n: sem(n) for n in names.split()}
        x_loaded = [s["x_loaded_0"], s["x_loaded_1"]]
        w_loaded = [s["w_loaded_0"], s["w_loaded_1"]]
        stored = [s["stored_0"], s["stored_1"]]

        x_t = x.rearrange("b (t p) d -> b t p d", p=P)
        out_t = out.rearrange("b (t p) d -> b t p d", p=P)
        adj_t = adjT.rearrange("b (t p) q -> b t p q", p=P)

        def at(b):
            return bass.ds(b, 1)

        def slot_of(kt, h):
            return kt % 2 * HG + h

        def staging(n):
            return ring[:, 4 * (n % 2):4 * (n % 2) + 2, :].rearrange("p a (c n) -> p (a c) n", n=D)

        def last_base():
            return chunks_before(ALL, B - 1, UNITS - 1, False) + 0

        def unit_no(b, up):
            return b * UNITS + up

        def x_landed(eng, b, first, use, t):
            before = QT if first else b * (3 * QT // 2) + QT // 2
            within = {"y": 0, "s": 0 if first else QT // 2, "n": QT // 2 if first else QT}[use]
            eng.wait_ge(x_loaded[t % 2], 16 * (before + within + t // 2 + 1))

        def chunk_no(b, up, first, last, kind, t):
            return chunks_before(ALL, b, up, first) + chunk_list(up, first, last).index((kind, t))

        def split_no(b, up, first, last, kind, t):
            here = chunk_list(up, first, last)
            return chunks_before(SPLIT, b, up, first) + count(SPLIT, here[:here.index((kind, t))])

        block = ctx.enter_context(nc.Block())

        @block.sync
        def _(sp):
            def load_x(b, t):
                sp.dma_start(x_in[:, t % 2, :], x_t[at(b), t].rearrange("a p d -> p (a d)")).then_inc(x_loaded[t % 2], 16)

            def restack(parity, kind):
                for h in range(HG):
                    for quarter, hl in enumerate({"q": (0, 1, 0, 1), "k": (0, 0, 1, 1)}[kind]):
                        sp.dma_start(stack[kind][quarter * DH:(quarter + 1) * DH, parity, h, :],
                                     part[kind][h * DH:(h + 1) * DH, hl, :]).then_inc(s["stack_loaded"], 16)

            def load_edges(b, t):
                sp.dma_start(edges[:], adj_t[at(b), t].rearrange("a p q -> p (a q)")).then_inc(s["edges_loaded"], 16)

            for n, wt in enumerate((Wq, Wk, Wv, Wo)):
                if n >= 2:
                    sp.wait_ge(s["w_lo_ready"], n - 1)
                sp.dma_start(staging(n), wt.rearrange("(c p) n -> p c n", p=P)).then_inc(w_loaded[n % 2], 16)
                if n == 1:
                    for m, bias in enumerate((bq, bk, bv)):
                        sp.dma_start(b_in[:, m, :], bias).then_inc(s["const_loaded"], 16)
                    sp.dma_start(bo_row[:], bo.partition_broadcast(P)).then_inc(s["const_loaded"], 16)
                    sp.dma_start(idt[:], ident).then_inc(s["const_loaded"], 16)
                    sp.dma_start(head1[:], headones).then_inc(s["const_loaded"], 16)
                    sp.dma_start(ones[:], rowones).then_inc(s["const_loaded"], 16)
            for t in range(QT):
                if t >= 2:
                    sp.wait_ge(s["x_stats"], t - 1)
                load_x(0, t)
            for t in range(QT):
                if t < 2:
                    sp.wait_ge(s["x_stats"], QT - 1 + t)
                else:
                    sp.wait_ge(s["chunk_ready"], t - 1)
                load_x(0, t)
                if t:
                    sp.wait_ge(s["mask_ready"], t)
                load_edges(0, t)
            for n, kind in enumerate("qk"):
                sp.wait_ge(s["chunk_free"], QT + 2 * n + 2)
                restack(0, kind)

            def graph(b, first, last):
                for up in range(UNITS):
                    U = unit_no(b, up)
                    slots = chunk_slots(up, first, last)
                    for m in range(2 * STEPS):
                        kind, t = slots.get(m, (" ", 0))
                        if up == 0 and not first:
                            if m < 2:
                                sp.wait_ge(s["chunk_ready"], chunks_before(ALL, b, 0, first) - len(PROJ) - 3 - 1 + m)
                                load_x(b - 1, m)
                            if kind == "y":
                                sp.wait_ge(s["y_ready"], (b - 1) * QT + t + 1)
                                sp.dma_start(out_t[at(b - 1), t].rearrange("a p d -> p (a d)"), y_out[:, t % 2, :]).then_inc(stored[t % 2], 16)
                                if t < QT - 2:
                                    load_x(b - 1, t + 2)
                        if kind in "qk" and t == 1:
                            sp.wait_ge(s["chunk_free"], chunk_no(b, up, first, last, kind, t) + 1)
                            restack((up + 1) % 2, kind)
                        if last:
                            continue
                        if up == 1 and m < 2:
                            if not first:
                                sp.wait_ge(s["y_ready"], b * QT - 1 + m)
                            else:
                                sp.wait_ge(s["chunk_ready"], QT - 1 + m)
                            load_x(b + 1, m)
                        if up == 2 and m < QT - 2:
                            sp.wait_ge(s["x_stats"], (b + 1) * QT + m + 1)
                            load_x(b + 1, m + 2)
                        if up == 2 and QT <= m < QT + 2:
                            sp.wait_ge(s["x_stats"], (b + 1) * QT + m - 1)
                            load_x(b + 1, m - QT)
                        if up == 2 and m == 2 * STEPS - 1:
                            sp.wait_ge(s["mask_ready"], (b + 1) * QT)
                            load_edges(b + 1, 0)
                        if up == UNITS - 1 and m % 2 == 0 and m:
                            sp.wait_ge(s["mask_ready"], (b + 1) * QT + m // 2)
                            load_edges(b + 1, m // 2)
                        if kind == "t" and t < QT - 2:
                            sp.wait_ge(s["chunk_ready"], chunk_no(b, up, first, last, "t", t) + 1)
                            load_x(b + 1, t + 2)

            graph(0, True, False)
            with sp.Fori(1, B - 1) as b:
                graph(b, False, False)
            graph(B - 1, False, True)
            for t in range(QT):
                if t < 2:
                    sp.wait_ge(s["y_ready"], (B - 1) * QT - 1 + t)
                    load_x(B - 1, t)
            for t in range(QT):
                sp.wait_ge(s["y_ready"], (B - 1) * QT + t + 1)
                sp.dma_start(out_t[B - 1, t], y_out[:, t % 2, :]).then_inc(stored[t % 2], 16)
                if t < QT - 2:
                    load_x(B - 1, t + 2)
            for k in range(2):
                sp.wait_ge(stored[k], 16 * B * QT // 2)

        @block.tensor
        def _(pe):
            def chunk(b, up, first, last, kind, t, hg):
                n = chunk_no(b, up, first, last, kind, t)
                emit_chunk(n, split_no(b, up, first, last, "k", 1) if kind == "n" else None, kind, t, hg, b, up)

            def emit_chunk(n, splits, kind, t, hg, b, up):
                if kind == "t":
                    pe.wait_ge(s["x_normed"], (b + 1) * QT + t + 1)
                if kind == "y":
                    pe.wait_ge(s["o_ready"], UNITS * b)
                if kind == "n":
                    pe.wait_ge(s["chunk_act"], splits + 1)
                if not (isinstance(n, int) and n == 0):
                    pe.wait_ge(s["chunk_free"], n)
                cols = slice(hg * P, (hg + 1) * P)
                if kind == "t":
                    for c in range(DC):
                        i = nc.tensor.transpose(misc[:, c * P:(c + 1) * P], x_in[:, t % 2, c * P:(c + 1) * P], idt[:])
                elif kind in "qk":
                    which = WQ if kind == "q" else WK
                    terms = [(w, h) for w, h in ((w_hi, hT_hi), (w_hi, hT_lo), (w_lo, hT_hi))]
                    for k, (w, h) in enumerate(terms):
                        for c in range(DC):
                            i = nc.tensor.matmul(misc, w[which][:, c, cols], h[:, c, t * HALF:(t + 1) * HALF],
                                                 start=k + c == 0, stop=k == 2 and c == DC - 1)
                elif kind == "v":
                    for tt in range(QT // 2):
                        tok = slice((t * QT // 2 + tt) * P, (t * QT // 2 + tt + 1) * P)
                        for k, (w, h) in enumerate(((w_hi, hT_hi), (w_lo, hT_hi), (w_hi, hT_lo))):
                            for c in range(DC):
                                i = nc.tensor.matmul(misc[:, tt * P:(tt + 1) * P], h[:, c, tok], w[WV][:, c, cols],
                                                     start=k + c == 0, stop=k == 2 and c == DC - 1)
                elif kind == "n":
                    for j in range(2):
                        for tt in range(QT):
                            i = nc.tensor.matmul(misc[:, (j * QT + tt) * HG:(j * QT + tt + 1) * HG],
                                                 squares[:, j, tt * P:(tt + 1) * P], head1[:], start=True, stop=True)
                elif kind == "y":
                    for k, (w, o) in enumerate(((w_hi, oT_hi), (w_lo, oT_hi), (w_hi, oT_lo))):
                        for c in range(DC):
                            i = nc.tensor.matmul(misc, o[:, c, t * P:(t + 1) * P], w[WO][:, c, :],
                                                 start=k + c == 0, stop=k == 2 and c == DC - 1)
                i.then_inc(s["chunk_ready"], 1)

            def scores(U, up, j):
                kt, h = divmod(j, HG)
                T = U * TILES + j
                if j == 0:
                    pe.wait_ge(s["stack_loaded"], 16 * 2 * HG * 4 * (U + 1))
                if not (isinstance(T, int) and T < 2):
                    pe.wait_ge(s["score_masked"], T - 1)
                for half in range(2):
                    i = nc.tensor.matmul(ps[:, 2 * (j % 2) + half, :], stack["k"][:, up % 2, h, kt * P:(kt + 1) * P],
                                         stack["q"][:, up % 2, h, half * HALF:(half + 1) * HALF], start=True, stop=True)
                i.then_inc(s["score_ready"], 1)

            def pv(U, up, kt, half, very_first):
                if half == 0:
                    pe.wait_ge(s["prob_ready"], U * TILES + HG * (kt + 1))
                if kt == 0 and half == 0 and not very_first:
                    pe.wait_ge(s["o_copied"], 2 * U)
                for h in range(HG):
                    i = nc.tensor.matmul(ps[h * DH:(h + 1) * DH, BANK_O + half, :], v_sb[:, up % 2, kt, h * DH:(h + 1) * DH],
                                         ring[:, slot_of(kt, h), half * HALF:(half + 1) * HALF], start=kt == 0, stop=kt == STEPS - 1,
                                         tile_position=(0, h * DH))
                i.then_inc(s["pv_done"], 1)

            def den(src, begin, end):
                for half in range(2):
                    for h in range(HG):
                        i = nc.tensor.matmul(ps[h * DH:(h + 1) * DH, BANK_D, :], ones[:, half, :], src(h, half),
                                             start=begin and half == 0, stop=end and half == 1, tile_position=(0, h * DH))
                i.then_inc(s["den_done"], 1)

            def in_ring(kt):
                return lambda h, half: ring[:, slot_of(kt, h), half * HALF:(half + 1) * HALF]

            def in_acc(h, half):
                return acc[:, h, half * HALF:(half + 1) * HALF]

            def tail(U, up, m):
                if m in (0, 2):
                    pv(U, up, STEPS - 1, m // 2, False)
                if m == 1:
                    pe.wait_ge(s["sum_done"], 16 * U + 16)
                    den(in_acc, False, False)
                if m == 3:
                    den(in_ring(STEPS - 1), False, True)

            def graph(b, first, last):
                for up in range(UNITS):
                    U = unit_no(b, up)
                    slots = chunk_slots(up, first, last)
                    for j in range(TILES):
                        kt, h = divmod(j, HG)
                        if j + 1 < TILES:
                            scores(U, up, j + 1)
                        elif not (last and up == UNITS - 1):
                            scores(U + 1, up + 1, 0)
                        if kt == 0 and not (first and up == 0):
                            tail(U - 1, (up + 1) % 2, j)
                        if kt and h % 2 == 0:
                            pv(U, up, kt - 1, h // 2, first and up == 0)
                        if kt == 4 and h == 3:
                            if not (first and up == 0):
                                pe.wait_ge(s["ln_done"], U)
                            pe.wait_ge(s["sum_done"], 16 * U + 8)
                            den(in_acc, True, False)
                        if kt == 7 and h == 3:
                            den(in_ring(STEPS - 2), False, False)
                        if j % 2 == 1 and j // 2 in slots:
                            kind, t = slots[j // 2]
                            chunk(b, up, first, last, kind, t, (up + 1) % UNITS)

            pe.wait_ge(s["const_loaded"], 16 * 7)
            for n, (kind, t) in enumerate(PRO_CHUNKS):
                if n == 0:
                    pe.wait_ge(s["w_lo_ready"], 4)
                emit_chunk(n, count(SPLIT, PRO_CHUNKS) - 1, kind, t, 0, -1, 0)
            scores(0, 0, 0)
            graph(0, True, False)
            with pe.Fori(1, B - 1) as b:
                graph(b, False, False)
            graph(B - 1, False, True)
            U = B * UNITS - 1
            for m in range(HG):
                tail(U, 1, m)
            base = last_base()
            for t in range(QT):
                emit_chunk(base + t, None, "y", t, 0, B, 0)

        @block.scalar
        def _(act):
            def exp(U, j):
                act.wait_ge(s["score_masked"], U * TILES + j + 1)
                r = ring[:, slot_of(*divmod(j, HG)), :]
                nc.scalar.activation(r, r, ACT.Exp, scale=SCALE / UP / UP).then_inc(s["prob_ready"], 1)

            def chunk(n, kind, t, up, hg, restacked, normed, spare):
                act.wait_ge(s["chunk_ready"], n + 1)
                half = slice(t * HALF, (t + 1) * HALF)
                if kind == "t":
                    nc.scalar.activation(hT_hi[:, :, t * P:(t + 1) * P], misc.rearrange("p (c n) -> p c n", n=P), ACT.Relu).then_inc(s["chunk_act"], 1)
                elif kind in "qk":
                    j = "qk".index(kind)
                    if normed is not None:
                        act.wait_ge(s["chunk_ready"], normed)
                    nc.scalar.activation(squares[:, j, half], misc, ACT.Square, bias=b_in[:, j, hg:hg + 1], scale=1 / UP)
                    if restacked is not None:
                        act.wait_ge(s["stack_loaded"], restacked)
                    nc.scalar.activation(part[kind][:, 0, half], misc, ACT.Identity, bias=b_up[:, j, hg:hg + 1]).then_inc(s["chunk_act"], 1)
                elif kind == "v":
                    if spare is not None:
                        act.wait_ge(s["pv_done"], spare)
                    nc.scalar.activation(v_sb[:, (up + 1) % 2, t * QT // 2:(t + 1) * QT // 2, :],
                                         misc.rearrange("p (c n) -> p c n", n=P), ACT.Copy).then_inc(s["chunk_free"], 1)

            def copy_o(U, half):
                if half == 0 and not (isinstance(U, int) and U == 0):
                    act.wait_ge(s["o_ready"], U)
                act.wait_ge(s["pv_done"], 16 * U + 15 + half)
                nc.scalar.activation(o_raw[:, half * HALF:(half + 1) * HALF], ps[:, BANK_O + half, :], ACT.Copy).then_inc(s["o_copied"], 1)

            def reciprocal(U):
                act.wait_ge(s["den_done"], 4 * U + 4)
                nc.scalar.activation(rden[:], ps[:, BANK_D, :], ACT.Ln).then_inc(s["ln_done"], 1)
                act.wait_ge(s["ln_done"], U + 1)
                nc.scalar.activation(rden[:], rden[:], ACT.Exp, scale=-1.0).then_inc(s["rden_ready"], 1)

            def o_high(U, c, y_read):
                act.wait_ge(s["o_scaled"], U + 1)
                if y_read is not None:
                    act.wait_ge(s["chunk_ready"], y_read)
                nc.scalar.activation(oT_hi[:, c, :], o_raw[:], ACT.Identity, bias=b_up[:, 2, c:c + 1]).then_inc(s["o_hi_ready"], 1)

            def rstds(g):
                act.wait_ge(s["x_mean"], g + 1)
                nc.scalar.activation(rstd[:], mv[:, :, 1], ACT.Ln, bias=eps[:]).then_inc(s["ln_var"], 1)
                act.wait_ge(s["ln_var"], g + 1)
                nc.scalar.activation(rstd[:], rstd[:], ACT.Exp, scale=-0.5).then_inc(s["rstd_ready"], 1)

            def graph(b, first, last):
                for up in range(UNITS):
                    U = unit_no(b, up)
                    slots = chunk_slots(up, first, last)
                    for j in range(TILES):
                        exp(U, j)
                        if not (first and up == 0):
                            if j in (1, 3):
                                copy_o(U - 1, j // 2)
                            if j == 4:
                                reciprocal(U - 1)
                            if j == 8:
                                y_read = None
                                if up == 1 and not first:
                                    y_read = chunk_no(b, 0, first, last, "y", QT - 1) + 1
                                o_high(U - 1, (up - 1) % UNITS, y_read)
                        if up == 2 and j == 24 and not last:
                            rstds(b + 1)
                        if j % 2 == 0 and j // 2 - 1 in slots:
                            kind, t = slots[j // 2 - 1]
                            if kind in "qkvt":
                                normed = restacked = spare = None
                                if kind in "qk":
                                    normed = chunk_no(b, up, first, last, "q", 0)
                                    restacked = 16 * 2 * HG * 4 * (U + 1)
                                if kind == "v" and not (first and up == 0):
                                    spare = 16 * U
                                chunk(chunk_no(b, up, first, last, kind, t), kind, t, up, (up + 1) % UNITS, restacked, normed, spare)

            nc.scalar.preload_act_table_set("natural_log_exp_and_others")
            for n in range(4):
                act.wait_ge(w_loaded[n % 2], 16 * (n // 2 + 1))
                nc.scalar.activation(w_hi[n][:], staging(n), ACT.Copy, scale=UP).then_inc(s["w_hi_ready"], 1)
            act.wait_ge(s["const_ready"], 4)
            rstds(0)
            for n, (kind, t) in enumerate(PRO_CHUNKS):
                if kind in "qkvt":
                    chunk(n, kind, t, -1, 0, None, None, None)
            graph(0, True, False)
            with act.Fori(1, B - 1) as b:
                graph(b, False, False)
            graph(B - 1, False, True)
            U = B * UNITS - 1
            for half in range(2):
                copy_o(U, half)
            reciprocal(U)
            o_high(U, UNITS - 1, None)

        @block.vector
        def _(dve):
            def masked(U, j, very_first):
                kt, h = divmod(j, HG)
                if not (very_first and kt < 2):
                    if h == 0:
                        dve.wait_ge(s["pv_done"], 16 * U + 2 * kt - 2)
                    if kt < 2:
                        if h == 0:
                            dve.wait_ge(s["den_done"], 4 * U + 2 * kt - 2)
                    else:
                        dve.wait_ge(s["sum_done"], 16 * U + {2: 0, 3: 0, 4: 4, 5: 8, 6: 8, 7: 12}[kt] + h + 1)
                dve.wait_ge(s["score_ready"], U * TILES + j + 1)
                nc.vector.tensor_tensor(ring[:, slot_of(kt, h), :], ps_s(j), mask[:, kt, :], ALU.add).then_inc(s["score_masked"], 1)

            def chunk(n, nsplit, kind, t, hg, g, xwait):
                dve.wait_ge(s["chunk_ready"], n + 1)
                half = slice(t * HALF, (t + 1) * HALF)
                if kind in "qkt":
                    dve.wait_ge(s["chunk_act"], nsplit + 1)
                if kind == "t":
                    nc.vector.scalar_tensor_tensor(out=hT_lo[:, :, t * P:(t + 1) * P], in0=misc.rearrange("p (c n) -> p c n", n=P), scalar=0.0,
                                                   in1=hT_hi[:, :, t * P:(t + 1) * P], op0=ALU.max, op1=ALU.subtract).then_inc(s["chunk_free"], 1)
                elif kind in "qk":
                    nc.vector.scalar_tensor_tensor(out=part[kind][:, 1, half], in0=misc, scalar=b_up[:, "qk".index(kind), hg:hg + 1],
                                                   in1=part[kind][:, 0, half], op0=ALU.add, op1=ALU.subtract).then_inc(s["chunk_free"], 1)
                elif kind == "n":
                    nc.vector.tensor_tensor(norms[:], misc[:, 0:2 * QT * HG], norms[:], ALU.max).then_inc(s["chunk_free"], 1)
                elif kind == "y":
                    dve.wait_ge(s["x_biased"], g * QT + t + 1)
                    if not (isinstance(g, int) and g == 0 and t < 2):
                        dve.wait_ge(stored[t % 2], 16 * (g * (QT // 2) + t // 2))
                    nc.vector.scalar_tensor_tensor(out=y_out[:, t % 2, :], in0=misc, scalar=1 / UP / UP, in1=x_in[:, t % 2, :],
                                                   op0=ALU.mult, op1=ALU.add).then_inc(s["y_ready"], 1)
                    dve.wait_ge(s["y_ready"], g * QT + t + 1)
                    nc.vector.memset(gap[:], 0.0).then_inc(s["chunk_free"], 1)

            def statistic(b, first, g, t):
                if b is None:
                    dve.wait_ge(x_loaded[t % 2], 16 * (t // 2 + 1))
                else:
                    x_landed(dve, b, first, "s", t)
                nc.vector.bn_stats(stats[:, t, :], x_in[:, t % 2, :]).then_inc(s["x_stats"], 1)

            def means(g):
                dve.wait_ge(s["x_stats"], (g + 1) * QT)
                nc.vector.memset(gap[:], 0.0)
                for t in range(QT):
                    i = nc.vector.bn_aggr(mv[:, t, :], stats[:, t, :])
                i.then_inc(s["x_mean"], 1)

            def normalise(b, first, g, t):
                if b is None:
                    dve.wait_ge(x_loaded[t % 2], 16 * (QT // 2 + t // 2 + 1))
                else:
                    x_landed(dve, b, first, "n", t)
                if t == 0:
                    dve.wait_ge(s["rstd_ready"], g + 1)
                nc.vector.tensor_scalar(x_in[:, t % 2, :], x_in[:, t % 2, :], mv[:, t, 0:1], rstd[:, t:t + 1],
                                        ALU.subtract, ALU.mult).then_inc(s["x_normed"], 1)

            def to_mask(g, kt):
                dve.wait_ge(s["edges_loaded"], 16 * (g * QT + kt + 1))
                nc.vector.tensor_scalar(mask[:, kt, :], edges[:], 0.0, MASKED, ALU.is_equal, ALU.mult).then_inc(s["mask_ready"], 1)

            def spread(U):
                dve.wait_ge(s["rden_ready"], U + 1)
                nc.vector.memset(gap[:], 0.0)
                for half in range(2):
                    nc.vector.stream_shuffle(rden_all[:, half * HALF:(half + 1) * HALF], rden[:], [half] * 32).then_inc(s["shuffled"], 1)

            def scale_o(U):
                dve.wait_ge(s["shuffled"], 2 * U + 2)
                dve.wait_ge(s["o_copied"], 2 * U + 2)
                nc.vector.tensor_tensor(o_raw[:], o_raw[:], rden_all[:], ALU.mult).then_inc(s["o_scaled"], 1)

            def o_low(U, c):
                dve.wait_ge(s["o_hi_ready"], U + 1)
                nc.vector.scalar_tensor_tensor(out=oT_lo[:, c, :], in0=o_raw[:], scalar=b_up[:, 2, c:c + 1], in1=oT_hi[:, c, :],
                                               op0=ALU.add, op1=ALU.subtract).then_inc(s["o_ready"], 1)

            def graph(b, first, last):
                for up in range(UNITS):
                    U = unit_no(b, up)
                    slots = chunk_slots(up, first, last)
                    for j in range(TILES):
                        kt, h = divmod(j, HG)
                        if up == 0 and j == 0:
                            dve.wait_ge(s["mask_ready"], (b + 1) * QT)
                        masked(U, j, first and up == 0)
                        if not (first and up == 0):
                            if j == 6:
                                spread(U - 1)
                            if j == 7:
                                scale_o(U - 1)
                            if j == 9:
                                o_low(U - 1, (up - 1) % UNITS)
                        if first and up == 0 and j in (12, 14, 16, 18):
                            n = (j - 12) // 2
                            nc.vector.tensor_reduce(limits[:, LIM_W + n:LIM_W + n + 1], w_hi[n][:], AX.XY, ALU.max, apply_absolute_value=True)\
                                .then_inc(s["limits_ready"], 1)
                        if first and up == 0 and j == 20:
                            nc.vector.tensor_reduce(limits[:, LIM_B:LIM_B + 1], b_up[:, 2, :], AX.X, ALU.max, apply_absolute_value=True)\
                                .then_inc(s["limits_ready"], 1)
                        if up == 2 and not last:
                            if j % 2 == 1 and j < 2 * QT:
                                statistic(b, first, b + 1, j // 2)
                            if j == 21:
                                means(b + 1)
                        if up == UNITS - 1 and not last:
                            if j % 2 == 0 and j < 2 * QT:
                                normalise(b, first, b + 1, j // 2)
                            if h == HG - 1:
                                dve.wait_ge(s["score_masked"], U * TILES + j + 1)
                                to_mask(b + 1, kt)
                        if j % 2 == 1 and (j - 3) // 2 in slots and j >= 3:
                            kind, t = slots[(j - 3) // 2]
                            if kind != "v":
                                n = chunk_no(b, up, first, last, kind, t)
                                ns = split_no(b, up, first, last, kind, t)
                                chunk(n, ns, kind, t, (up + 1) % UNITS, b - 1 if kind == "y" else None, None)

            nc.vector.memset(eps[:], EPS).then_inc(s["const_ready"], 1)
            nc.vector.memset(norms[:], 0.0).then_inc(s["const_ready"], 1)
            for n in range(4):
                dve.wait_ge(s["w_hi_ready"], n + 1)
                nc.vector.scalar_tensor_tensor(out=w_lo[n][:], in0=staging(n), scalar=UP, in1=w_hi[n][:], op0=ALU.mult, op1=ALU.subtract)\
                    .then_inc(s["w_lo_ready"], 1)
            dve.wait_ge(s["const_loaded"], 16 * 7)
            nc.vector.tensor_scalar(b_up[:], b_in[:], UP, None, ALU.mult).then_inc(s["const_ready"], 1)
            nc.vector.memset(gap[:], 0.0).then_inc(s["const_ready"], 1)
            dve.wait_ge(s["const_ready"], 4)
            for t in range(QT):
                statistic(None, True, 0, t)
            means(0)
            for n, (kind, t) in enumerate(PRO_CHUNKS):
                if kind == "t":
                    normalise(None, True, 0, t)
                    to_mask(0, t)
                if kind != "v":
                    chunk(n, count(SPLIT, PRO_CHUNKS[:n]), kind, t, 0, None, None)
            graph(0, True, False)
            with dve.Fori(1, B - 1) as b:
                graph(b, False, False)
            graph(B - 1, False, True)
            U = B * UNITS - 1
            spread(U)
            scale_o(U)
            o_low(U, UNITS - 1)
            base = last_base()
            for t in range(QT):
                chunk(base + t, None, "y", t, 0, B - 1, None)
            nc.vector.tensor_reduce(limits[:, LIM_N:LIM_QK].rearrange("p (j h) -> p j h", j=2), norms[:].rearrange("p (j t h) -> p j h t", j=2, t=QT),
                                    AX.X, ALU.max).then_inc(s["limits_ready"], 1)
            dve.wait_ge(s["limits_everywhere"], 1)
            nc.vector.scalar_tensor_tensor(out=limits[:, LIM_QK:LIMITS], in0=limits[:, LIM_N:LIM_N + HG], scalar=SCALE * SCALE,
                                           in1=limits[:, LIM_N + HG:LIM_QK], op0=ALU.mult, op1=ALU.mult).then_inc(s["verdict_step"], 1)
            nc.vector.tensor_scalar(limits[:, LIM_W:LIM_W + 4], limits[:, LIM_W:LIM_W + 4], BOUND_SQ / (W_MAX * UP), None, ALU.mult)\
                .then_inc(s["verdict_step"], 1)
            dve.wait_ge(s["verdict_step"], 2)
            nc.vector.reduce_max(largest[:], limits[:], AX.X).then_inc(s["verdict_step"], 1)
            dve.wait_ge(s["verdict_step"], 3)
            nc.vector.tensor_scalar(flag[:], largest[0:1, :], BOUND_SQ, None, ALU.is_gt).then_inc(s["verdict_step"], 1)

        @block.gpsimd
        def _(pool):
            def sums(U, kt, h, very_first):
                group, k = divmod(kt, 3)
                pool.wait_ge(s["prob_ready"], U * TILES + HG * kt + h + 1)
                if k == 1 and h == 0:
                    if group == 1:
                        pool.wait_ge(s["den_done"], 4 * U + 1)
                    elif not very_first:
                        pool.wait_ge(s["den_done"], 4 * U - 1)
                first = ring[:, slot_of(kt - 1, h), :] if k == 1 else acc[:, h, :]
                nc.gpsimd.tensor_tensor(acc[:, h, :], first, ring[:, slot_of(kt, h), :], ALU.add).then_inc(s["sum_done"], 1)

            def bias_x(b, first, g, t):
                if b is None:
                    pool.wait_ge(x_loaded[t % 2], 16 * (B * (3 * QT // 2) - QT // 2 + t // 2 + 1))
                else:
                    x_landed(pool, b, first, "y", t)
                nc.gpsimd.tensor_tensor(x_in[:, t % 2, :], x_in[:, t % 2, :], bo_row[:], ALU.add).then_inc(s["x_biased"], 1)

            def graph(b, first, last):
                for up in range(UNITS):
                    U = unit_no(b, up)
                    for kt in range(STEPS):
                        if up == 0 and not first:
                            for t in {1: (0, 1), 2: (), 3: (2,), 4: (3, 4), 5: (5, 6), 6: (7,)}.get(kt, ()):
                                bias_x(b, first, b - 1, t)
                        if kt in (1, 2, 4, 5):
                            for h in range(HG):
                                sums(U, kt, h, first and up == 0)

            pool.wait_ge(s["const_loaded"], 16 * 7)
            graph(0, True, False)
            with pool.Fori(1, B - 1) as b:
                graph(b, False, False)
            graph(B - 1, False, True)
            for t in range(QT):
                bias_x(None, False, B - 1, t)
            pool.wait_ge(s["limits_ready"], 6)
            nc.gpsimd.partition_all_reduce(limits[:, 0:LIM_QK], limits[:, 0:LIM_QK], P, RMAX).then_inc(s["limits_everywhere"], 1)


def program(nc, x, adj, adjT, Wq, bq, Wk, bk, Wv, bv, bv_cols, Wo, bo, ident, headones, rowones, out):
    scratch = [nc.dram_tensor(n, shape, F32, kind="Internal").ap()
               for n, shape in (("qT_s", [B, D, S]), ("kT_s", [B, D, S]), ("v_s", [B, S, D]), ("o_s", [B, S, D]))]
    with nc.sbuf_tensor("flag", [1, 1], I32) as flag:
        fast_attention(nc, x, adjT, Wq, bq, Wk, bk, Wv, bv_cols, Wo, bo, ident, headones, rowones, out, flag)
        general_attention(nc, flag[0:1, 0:1], x, adj, Wq, bq, Wk, bk, Wv, bv, Wo, bo, ident, out, scratch)


def kernel(x, adj, L0_gnn_Wq, L0_gnn_bq, L0_gnn_Wk, L0_gnn_bk, L0_gnn_Wv, L0_gnn_bv, L0_gnn_Wo, L0_gnn_bo):
    import numpy as np
    import concourse.bacc as bacc
    from concourse.bass_utils import run_bass_kernel_spmd

    nc = bacc.Bacc("TRN2", target_bir_lowering=False, num_devices=1)
    heads = np.arange(P)[:, None] // DH == np.arange(HG)
    rows = np.broadcast_to(np.arange(DH) % 2 == np.arange(2)[:, None], (P, 2, DH))
    arrays = {
        "x": x, "adj": adj, "adjT": np.swapaxes(np.asarray(adj), 1, 2),
        "Wq": L0_gnn_Wq, "bq": np.asarray(L0_gnn_bq).reshape(DC, P).T, "Wk": L0_gnn_Wk, "bk": np.asarray(L0_gnn_bk).reshape(DC, P).T,
        "Wv": L0_gnn_Wv, "bv": L0_gnn_bv, "bv_cols": np.asarray(L0_gnn_bv).reshape(DC, P).T, "Wo": L0_gnn_Wo, "bo": L0_gnn_bo,
        "ident": np.eye(P, dtype=np.float32), "headones": heads.astype(mybir.dt.np(BF16)), "rowones": rows.astype(np.float32),
    }
    arrays = {n: np.ascontiguousarray(a) for n, a in arrays.items()}
    args = [nc.dram_tensor(n, a.shape, mybir.dt.from_np(a.dtype), kind="ExternalInput").ap() for n, a in arrays.items()]
    out = nc.dram_tensor("out", (B, S, D), F32, kind="ExternalOutput").ap()
    program(nc, *args, out)
    r = run_bass_kernel_spmd(nc, [arrays], core_ids=[0])
    return r.results[0]["out"]
```

```python
import concourse.bass as bass
from concourse import mybir
from contextlib import ExitStack

B, S, D, H, P = 8, 1024, 512, 16, 128
DH = D // H
DC = D // P
QT = S // P
HG = P // DH
SCALE = float(DH) ** -0.5
EPS = 1e-5
MASKED = -1e30

F32 = mybir.dt.float32
I32 = mybir.dt.int32
ALU = mybir.AluOpType
ACT = mybir.ActivationFunctionType
AX = mybir.AxisListType


def general_attention(nc, flag, x, adj, Wq, bq, Wk, bk, Wv, bv, Wo, bo, ident, out, scratch):
    qT_s, kT_s, v_s, o_s = scratch
    ctx = ExitStack()
    with ctx:
        def sb(name, shape, dt=F32):
            return ctx.enter_context(nc.sbuf_tensor("g_" + name, shape, dt))

        def sem(name):
            return ctx.enter_context(nc.semaphore("g_" + name))

        w = [sb(n, [P, DC, D]) for n in ("wq", "wk", "wv", "wo")]
        bqk = [sb(n, [P, DC]) for n in ("bq", "bk")]
        bv_row, bo_row = sb("bv_row", [P, D]), sb("bo_row", [P, D])
        idt = sb("ident", [P, P])
        x_in = sb("x_in", [P, D])
        stats, mv = sb("stats", [P, 6]), sb("mv", [P, 2])
        lnv, rstd = sb("lnv", [P, 1]), sb("rstd", [P, 1])
        eps = sb("eps", [P, 1])
        xn = sb("xn", [P, D])
        hT = sb("hT", [P, DC, P])
        qkT = [sb(n, [P, DC, P]) for n in ("qT", "kT")]
        v_out = sb("v_out", [P, D])
        edges = sb("edges", [P, QT, S], I32)
        bias = sb("bias", [P, QT, S])
        qT, kT = sb("qT_h", [DH, S]), sb("kT_h", [DH, S])
        v = sb("v_h", [P, QT, DH])
        masked = sb("masked", [P, S])
        rowmax, shift = sb("rowmax", [P, 1]), sb("shift", [P, 1])
        prob = sb("prob", [P, S])
        rowsum, rinv = sb("rowsum", [P, 1]), sb("rinv", [P, 1])
        probT = sb("probT", [P, QT, P])
        o_h = sb("o_h", [P, QT, DH])
        o_in, oT = sb("o_in", [P, D]), sb("oT", [P, DC, P])
        y, y_out = sb("y", [P, D]), sb("y_out", [P, D])

        ps = ctx.enter_context(nc.psum_tensor("g_ps", [P, 8, 512], F32))
        ps_t = ps[:, 0, :].rearrange("p (c n) -> p c n", c=DC)
        ps_q = [ps[:, 1 + j, :].rearrange("p (c n) -> p c n", c=DC) for j in range(2)]
        ps_v = ps[:, 3, :]
        ps_s = ps[:, 4:6, :].rearrange("p a n -> p (a n)")
        ps_pt = ps[:, 6:8, :].rearrange("p a (k n) -> p (a k) n", n=P)
        ps_o = ps[:, 2, 0:DH]
        ps_y = ps[:, 1, :]

        masked_ready = sem("masked_ready")
        gap = sb("gap", [P, 1])
        loaded, eps_set = sem("loaded"), sem("eps_set")
        x_loaded, mv_ready, stats_ready, ln_ready, rstd_ready, xn_ready, xT_ready, hT_ready, proj_ready, proj_copied, qkv_stored = (
            sem(n) for n in ("x_loaded", "mv_ready", "stats_ready", "ln_ready", "rstd_ready", "xn_ready", "xT_ready", "hT_ready",
                             "proj_ready", "proj_copied", "qkv_stored"))
        edges_loaded, bias_ready, head_loaded = sem("edges_loaded"), sem("bias_ready"), sem("head_loaded")
        score_ready, max_ready, shift_ready, prob_ready, probT_ready, probT_copied, o_ready, rinv_ready, o_copied, o_stored = (
            sem(n) for n in ("score_ready", "max_ready", "shift_ready", "prob_ready", "probT_ready", "probT_copied", "o_ready",
                             "rinv_ready", "o_copied", "o_stored"))
        o_loaded, oT_ready, oT_copied, y_ready, y_biased, y_done, y_stored = (
            sem(n) for n in ("o_loaded", "oT_ready", "oT_copied", "y_ready", "y_biased", "y_done", "y_stored"))

        WEIGHTS = 16 * 9
        TOKT = B * QT
        x_t = x.rearrange("b (t p) d -> (b t) p d", p=P)
        out_t = out.rearrange("b (t p) d -> (b t) p d", p=P)
        v_t = v_s.rearrange("b (t p) d -> (b t) p d", p=P)
        o_t = o_s.rearrange("b (t p) d -> (b t) p d", p=P)
        qk_t = [s.rearrange("b (c p) (t n) -> b t p c n", p=P, n=P) for s in (qT_s, kT_s)]

        block = ctx.enter_context(nc.Block())

        def gated(eng, program):
            wanted = eng.value_load(flag, min_val=0, max_val=1)
            with eng.If(wanted > 0):
                program()

        @block.sync
        def _(sp):
            def program():
                for n, wt in enumerate((Wq, Wk, Wv, Wo)):
                    sp.dma_start(w[n][:], wt.rearrange("(c p) n -> p c n", p=P)).then_inc(loaded, 16)
                for n, bias_ in enumerate((bq, bk)):
                    sp.dma_start(bqk[n][:], bias_).then_inc(loaded, 16)
                sp.dma_start(bv_row[:], bv.partition_broadcast(P)).then_inc(loaded, 16)
                sp.dma_start(bo_row[:], bo.partition_broadcast(P)).then_inc(loaded, 16)
                sp.dma_start(idt[:], ident).then_inc(loaded, 16)
                with sp.Fori(0, B) as b:
                    for t in range(QT):
                        i = b * QT + t
                        sp.dma_start(x_in[:], x_t[bass.ds(i, 1)].rearrange("a p d -> p (a d)")).then_inc(x_loaded, 16)
                        sp.wait_ge(proj_copied, 3 * i + 3)
                        for n in range(2):
                            sp.dma_start(qk_t[n][bass.ds(b, 1), t].rearrange("a p c n -> p (a c) n"), qkT[n][:]).then_inc(qkv_stored, 16)
                        sp.dma_start(v_t[bass.ds(i, 1)].rearrange("a p d -> p (a d)"), v_out[:]).then_inc(qkv_stored, 16)
                sp.wait_ge(qkv_stored, 48 * TOKT)
                with sp.Fori(0, B) as b:
                    sp.dma_start(edges[:], adj[bass.ds(b, 1)].rearrange("a (t p) k -> p (a t) k", p=P)).then_inc(edges_loaded, 16)
                    with sp.Fori(0, H) as h:
                        u = b * H + h
                        sp.dma_start(qT[:], qT_s[bass.ds(b, 1), bass.ds(h * DH, DH)].rearrange("a p n -> p (a n)")).then_inc(head_loaded, 16)
                        sp.dma_start(kT[:], kT_s[bass.ds(b, 1), bass.ds(h * DH, DH)].rearrange("a p n -> p (a n)")).then_inc(head_loaded, 16)
                        sp.dma_start(v[:], v_s[bass.ds(b, 1), :, bass.ds(h * DH, DH)].rearrange("a (t p) n -> p (a t) n", p=P)).then_inc(head_loaded, 16)
                        sp.wait_ge(o_copied, QT * u + QT)
                        sp.dma_start(o_s[bass.ds(b, 1), :, bass.ds(h * DH, DH)].rearrange("a (t p) n -> p (a t) n", p=P), o_h[:]).then_inc(o_stored, 16)
                sp.wait_ge(o_stored, 16 * B * H)
                with sp.Fori(0, TOKT) as i:
                    sp.dma_start(o_in[:], o_t[bass.ds(i, 1)].rearrange("a p d -> p (a d)")).then_inc(o_loaded, 16)
                    sp.dma_start(x_in[:], x_t[bass.ds(i, 1)].rearrange("a p d -> p (a d)")).then_inc(o_loaded, 16)
                    sp.wait_ge(y_done, i + 1)
                    sp.dma_start(out_t[bass.ds(i, 1)].rearrange("a p d -> p (a d)"), y_out[:]).then_inc(y_stored, 16)
                sp.wait_ge(y_stored, 16 * TOKT)
            gated(sp, program)

        @block.vector
        def _(dve):
            def program():
                nc.vector.memset(eps[:], EPS).then_inc(eps_set, 1)
                dve.wait_ge(loaded, WEIGHTS)
                with dve.Fori(0, TOKT) as i:
                    dve.wait_ge(x_loaded, 16 * i + 16)
                    nc.vector.bn_stats(stats[:], x_in[:]).then_inc(stats_ready, 1)
                    dve.wait_ge(stats_ready, i + 1)
                    nc.vector.memset(gap[:], 0.0)
                    nc.vector.bn_aggr(mv[:], stats[:]).then_inc(mv_ready, 1)
                    dve.wait_ge(rstd_ready, i + 1)
                    nc.vector.tensor_scalar(xn[:], x_in[:], mv[:, 0:1], rstd[:], ALU.subtract, ALU.mult).then_inc(xn_ready, 1)
                    dve.wait_ge(proj_ready, i + 1)
                    for n in range(2):
                        for m in range(DC):
                            last = nc.vector.tensor_scalar(qkT[n][:, m, :], ps_q[n][:, m, :], bqk[n][:, m:m + 1], None, ALU.add)
                        last.then_inc(proj_copied, 1)
                    nc.vector.tensor_tensor(v_out[:], ps_v, bv_row[:], ALU.add).then_inc(proj_copied, 1)
                    dve.wait_ge(qkv_stored, 48 * i + 48)
                with dve.Fori(0, B) as b:
                    dve.wait_ge(edges_loaded, 16 * b + 16)
                    nc.vector.tensor_scalar(bias[:], edges[:], 0.0, MASKED, ALU.is_equal, ALU.mult).then_inc(bias_ready, 1)
                    dve.wait_ge(bias_ready, b + 1)
                    nc.vector.memset(gap[:], 0.0)
                    with dve.Fori(0, H) as h:
                        for t in range(QT):
                            n = (b * H + h) * QT + t
                            dve.wait_ge(score_ready, n + 1)
                            nc.vector.tensor_tensor(masked[:], ps_s, bias[:, t, :], ALU.add).then_inc(masked_ready, 1)
                            dve.wait_ge(masked_ready, n + 1)
                            nc.vector.reduce_max(rowmax[:], masked[:], AX.X).then_inc(max_ready, 1)
                            dve.wait_ge(max_ready, n + 1)
                            nc.vector.tensor_scalar(shift[:], rowmax[:], -SCALE, None, ALU.mult).then_inc(shift_ready, 1)
                            dve.wait_ge(probT_ready, n + 1)
                            nc.vector.tensor_copy(probT[:], ps_pt).then_inc(probT_copied, 1)
                            nc.vector.reciprocal(rinv[:], rowsum[:]).then_inc(rinv_ready, 1)
                            dve.wait_ge(rinv_ready, n + 1)
                            dve.wait_ge(o_ready, n + 1)
                            nc.vector.tensor_scalar(o_h[:, t, :], ps_o, rinv[:], None, ALU.mult).then_inc(o_copied, 1)
                        dve.wait_ge(o_stored, 16 * (b * H + h) + 16)
                with dve.Fori(0, TOKT) as i:
                    dve.wait_ge(o_loaded, 32 * i + 32)
                    dve.wait_ge(oT_ready, i + 1)
                    nc.vector.tensor_copy(oT[:], ps_t).then_inc(oT_copied, 1)
                    dve.wait_ge(y_ready, i + 1)
                    nc.vector.tensor_tensor(y[:], ps_y, bo_row[:], ALU.add).then_inc(y_biased, 1)
                    dve.wait_ge(y_biased, i + 1)
                    nc.vector.tensor_tensor(y_out[:], y[:], x_in[:], ALU.add).then_inc(y_done, 1)
                    dve.wait_ge(y_stored, 16 * i + 16)
            gated(dve, program)

        @block.scalar
        def _(act):
            def program():
                act.wait_ge(eps_set, 1)
                with act.Fori(0, TOKT) as i:
                    act.wait_ge(mv_ready, i + 1)
                    nc.scalar.activation(lnv[:], mv[:, 1:2], ACT.Ln, bias=eps[:]).then_inc(ln_ready, 1)
                    act.wait_ge(ln_ready, i + 1)
                    nc.scalar.activation(rstd[:], lnv[:], ACT.Exp, scale=-0.5).then_inc(rstd_ready, 1)
                    act.wait_ge(xT_ready, i + 1)
                    nc.scalar.activation(hT[:], ps_t, ACT.Relu).then_inc(hT_ready, 1)
                with act.Fori(0, B * H) as u:
                    for t in range(QT):
                        n = u * QT + t
                        act.wait_ge(shift_ready, n + 1)
                        nc.scalar.activation(prob[:], masked[:], ACT.Exp, bias=shift[:], scale=SCALE, accum_out=rowsum[:]).then_inc(prob_ready, 1)
            gated(act, program)

        @block.tensor
        def _(pe):
            def program():
                pe.wait_ge(loaded, WEIGHTS)
                with pe.Fori(0, TOKT) as i:
                    pe.wait_ge(xn_ready, i + 1)
                    for c in range(DC):
                        last = nc.tensor.transpose(ps_t[:, c, :], xn[:, c * P:(c + 1) * P], idt[:])
                    last.then_inc(xT_ready, 1)
                    pe.wait_ge(hT_ready, i + 1)
                    for n in range(2):
                        for m in range(DC):
                            for c in range(DC):
                                nc.tensor.matmul(ps_q[n][:, m, :], w[n][:, c, m * P:(m + 1) * P], hT[:, c, :], start=c == 0, stop=c == DC - 1)
                    for c in range(DC):
                        last = nc.tensor.matmul(ps_v, hT[:, c, :], w[2][:, c, :], start=c == 0, stop=c == DC - 1)
                    last.then_inc(proj_ready, 1)
                with pe.Fori(0, B * H) as u:
                    pe.wait_ge(head_loaded, 48 * u + 48)
                    for t in range(QT):
                        n = u * QT + t
                        for half in range(2):
                            last = nc.tensor.matmul(ps[:, 4 + half, :], qT[:, t * P:(t + 1) * P], kT[:, half * 512:(half + 1) * 512], start=True, stop=True)
                        last.then_inc(score_ready, 1)
                        pe.wait_ge(prob_ready, n + 1)
                        for k in range(QT):
                            last = nc.tensor.transpose(ps_pt[:, k, :], prob[:, k * P:(k + 1) * P], idt[:])
                        last.then_inc(probT_ready, 1)
                        pe.wait_ge(probT_copied, n + 1)
                        for k in range(QT):
                            last = nc.tensor.matmul(ps_o, probT[:, k, :], v[:, k, :], start=k == 0, stop=k == QT - 1)
                        last.then_inc(o_ready, 1)
                with pe.Fori(0, TOKT) as i:
                    pe.wait_ge(o_loaded, 32 * i + 32)
                    for c in range(DC):
                        last = nc.tensor.transpose(ps_t[:, c, :], o_in[:, c * P:(c + 1) * P], idt[:])
                    last.then_inc(oT_ready, 1)
                    pe.wait_ge(oT_copied, i + 1)
                    for c in range(DC):
                        last = nc.tensor.matmul(ps_y, oT[:, c, :], w[3][:, c, :], start=c == 0, stop=c == DC - 1)
                    last.then_inc(y_ready, 1)
            gated(pe, program)


F16 = mybir.dt.float16
BF16 = mybir.dt.bfloat16
HALF = 512
UNITS = D // P
STEPS = QT
TILES = STEPS * HG
UP = 64.0
STACKED = 16 * 2 * P // DH
RING = 2 * HG
W_MAX = 120.0 / UP
LIM_W, LIM_B, LIM_N, LIM_QK = 0, 4, 5, 5 + 2 * HG
LIMITS = LIM_QK + HG
RMAX = bass.bass_isa.ReduceOp.max
BOUND_SQ = 36.0 ** 2 * 0.96

PROJ = [("q", 0), ("q", 1), ("k", 0), ("k", 1), ("v", 0), ("v", 1)]
NORMS = ("n", 0)


def chunk_plan(up, first, last):
    if up == UNITS - 1:
        if last:
            return []
        kinds = [("t", t) for t in range(QT)]
        plan = [(1 + 3 * t // 2, 1, *c) for t, c in enumerate(kinds)]
        at = plan[-1][0] + 1
        return plan + [(at + 1 + 3 * n, 2, *c) for n, c in enumerate(PROJ[:5])] + [(at + 16, 1, *PROJ[5]), (at + 17, 1, *NORMS)]
    if up in (0, 1) and not first:
        if up == 0:
            kinds = PROJ[:4] + [("y", 0), ("y", 1), PROJ[4], ("y", 2), PROJ[5], ("y", 3)]
        else:
            kinds = [("y", 4), PROJ[0], ("y", 5), PROJ[1], ("y", 6), PROJ[2], ("y", 7), PROJ[3], PROJ[4], PROJ[5]]
        lengths = [3] * 8 + [2, 3] if up == 0 else [3] * 8 + [2, 2]
        plan = [(sum(lengths[:n]) + (lengths[n] > 2), min(2, lengths[n]), *c) for n, c in enumerate(kinds)]
    else:
        plan = [(1 + 4 * n, 3, *c) for n, c in enumerate(PROJ)]
    return plan + [(29, 1, *NORMS)]


def chunk_list(up, first, last):
    return [c[2:] for c in chunk_plan(up, first, last)]


def chunks_ending(up, first, last):
    return {at + n - 1: (kind, t) for at, n, kind, t in chunk_plan(up, first, last)}


OUTPUT_AT = {t: up * TILES + j for up in (0, 1) for j, (kind, t) in chunks_ending(up, False, False).items() if kind == "y"}
WEIGHTS_AFTER = {("t", 3): 2, ("t", 7): 3}
SQUARES_AT = {25: ("q", 0), 26: ("q", 1), 27: ("k", 0), 28: ("k", 1)}


PRO_CHUNKS = [("t", n) for n in range(QT)] + PROJ + [NORMS]
ALL = "qkvtyn"
SPLIT = "qkt"


def count(kinds, chunks):
    return sum(c[0] in kinds for c in chunks)


def chunks_before(kinds, b, up, first):
    n = count(kinds, PRO_CHUNKS)
    here = sum(count(kinds, chunk_list(k, first, False)) for k in range(up))
    if first:
        return n + here
    zero = sum(count(kinds, chunk_list(k, True, False)) for k in range(UNITS))
    each = sum(count(kinds, chunk_list(k, False, False)) for k in range(UNITS))
    return (b * each + (n + zero - each)) + here


def fast_attention(nc, x, adjT, Wq, bq, Wk, bk, Wv, bv, Wo, bo, ident, headones, rowones, out, parts, flag):
    ctx = ExitStack()
    with ctx:
        def sb(name, shape, dt=F32):
            return ctx.enter_context(nc.sbuf_tensor(name, shape, dt))

        def sem(name):
            return ctx.enter_context(nc.semaphore(name))

        w_hi = [sb(f"w{n}_hi", [P, DC, D], F16) for n in "qkvo"]
        w_lo = [sb(f"w{n}_lo", [P, DC, D], F16) for n in "qkvo"]
        WQ, WK, WV, WO = range(4)
        b_in = sb("b_in", [P, 3, DC])
        b_up = sb("b_up", [P, 3, DC])
        bo_row = sb("bo_row", [P, D])
        idt = sb("idt", [P, P])
        head1 = sb("head1", [P, HG], BF16)
        ones = sb("ones", [P, 2, DH])
        eps = sb("eps", [P, 1])
        gap = sb("gap", [P, 1])
        limits = sb("limits", [P, LIMITS])
        largest = sb("largest", [P, 1])
        mask = sb("mask", [P, QT, S], BF16)
        edges = sb("edges", [P, S], I32)
        hT_hi, hT_lo = sb("hT_hi", [P, DC, S], F16), sb("hT_lo", [P, DC, S], F16)
        oT_hi, oT_lo = sb("oT_hi", [P, DC, S], F16), sb("oT_lo", [P, DC, S], F16)
        x_in = sb("x_in", [P, 2, D])
        stats, mv = sb("stats", [P, QT, 6]), sb("mv", [P, QT, 2])
        rstd = sb("rstd", [P, QT])
        y_out = sb("y_out", [P, 2, D])
        part = {c: sb(f"{c}_part", [P, 2, S], F16) for c in "qk"}
        full = sb("full", [P, 2, HALF])
        squares = sb("squares", [P, 2, S], BF16)
        norms = sb("norms", [P, 2 * QT * HG])
        stack = {c: sb(f"{c}_stack", [P, 2, HG, S], F16) for c in "qk"}
        v_sb = sb("v_sb", [P, 2, QT, P])
        ring = sb("ring", [P, RING, S])
        acc = sb("acc", [P, HG, S])
        o_raw = sb("o_raw", [P, S])
        rden = squares[:].rearrange("p j n -> p (j n)").bitcast(F32)[:, 0:HALF]
        rden_all = sb("rden_all", [P, S])

        ps = ctx.enter_context(nc.psum_tensor("ps", [P, 8, HALF], F32))
        BANK_O, BANK_D, BANK_M = 4, 6, 7
        ps_o = ps[:, BANK_O:BANK_O + 2, :].rearrange("p a n -> p (a n)")
        misc = ps[:, BANK_M, :]

        EARLY_BANKS = 4

        def early_bank(n):
            return ps[:, BANK_O + n % EARLY_BANKS, :]

        def ps_s(j):
            return ps[:, 2 * (j % 2):2 * (j % 2) + 2, :].rearrange("p a n -> p (a n)")

        names = ("squared w_loaded_0 w_loaded_1 q_stored k_stored w_hi_ready w_lo_ready const_ready const_loaded x_loaded_0 x_loaded_1 edges_loaded stack_loaded stored_0 stored_1 "
                 "chunk_ready high_ready low_ready chunk_free score_ready score_masked prob_ready pv_done sum_done den_done "
                 "o_copied ln_done rden_ready o_scaled o_hi_ready o_ready shuffled mask_ready x_stats x_mean ln_var rstd_ready "
                 "x_normed x_biased y_ready limits_ready limits_everywhere verdict_step")
        s = {n: sem(n) for n in names.split()}
        x_loaded = [s["x_loaded_0"], s["x_loaded_1"]]
        w_loaded = [s["w_loaded_0"], s["w_loaded_1"]]
        stored = [s["stored_0"], s["stored_1"]]

        x_t = x.rearrange("b (t p) d -> b t p d", p=P)
        out_t = out.rearrange("b (t p) d -> b t p d", p=P)
        adj_t = adjT.rearrange("b (t p) q -> b t p q", p=P)

        def at(b):
            return bass.ds(b, 1)

        def slot_of(kt, h):
            return kt % 2 * HG + h

        def staging(n):
            return ring[:, 4 * (n % 2):4 * (n % 2) + 2, :].rearrange("p a (c n) -> p (a c) n", n=D)

        def x_first(t):
            return ring[:, (2, 3, 6, 7)[t // 2], t % 2 * D:(t % 2 + 1) * D]

        def x_last(t):
            return acc[:, t // 2, t % 2 * D:(t % 2 + 1) * D]

        def last_base():
            return chunks_before(ALL, B - 1, UNITS - 1, False)

        def unit_no(b, up):
            return b * UNITS + up

        def x_landed(eng, b, first, use, t):
            before = 1 if first else b * (3 * QT // 2) + 1 - QT // 2
            within = {"y": 0, "s": 0 if first else QT // 2, "n": QT // 2 if first else QT}[use]
            eng.wait_ge(x_loaded[t % 2], 16 * (before + within + t // 2 + 1))

        def chunk_no(b, up, first, last, kind, t):
            return chunks_before(ALL, b, up, first) + chunk_list(up, first, last).index((kind, t))

        def split_no(b, up, first, last, kind, t):
            here = chunk_list(up, first, last)
            return chunks_before(SPLIT, b, up, first) + count(SPLIT, here[:here.index((kind, t))])

        def split_parity(up, first, last, kind, t):
            if kind not in SPLIT:
                return None
            return split_no(0 if first else 2, up, first, last, kind, t) % 2

        def o_high_at(up, first):
            return 24 if up == 1 and not first else 20 if up == 3 else 9

        block = ctx.enter_context(nc.Block())

        @block.sync
        def _(sp):
            def load_x(b, t):
                sp.dma_start(x_in[:, t % 2, :], x_t[at(b), t].rearrange("a p d -> p (a d)")).then_inc(x_loaded[t % 2], 16)

            def store_parts(kind):
                sp.dma_start(parts[kind], part[kind][:]).then_inc(s[kind + "_stored"], 16)

            def load_stack(U, parity, kind):
                sp.wait_ge(s[kind + "_stored"], 16 * (U + 1))
                for quarter, hl in enumerate({"q": (0, 1, 0, 1), "k": (0, 0, 1, 1)}[kind]):
                    sp.dma_start(stack[kind][quarter * DH:(quarter + 1) * DH, parity, :, :],
                                 parts[kind][:, hl, :].rearrange("(h p) n -> p h n", h=HG)).then_inc(s["stack_loaded"], 16)

            def load_edges(b, t):
                sp.dma_start(edges[:], adj_t[at(b), t].rearrange("a p q -> p (a q)")).then_inc(s["edges_loaded"], 16)

            def load_weights(n):
                if n >= 2:
                    sp.wait_ge(s["w_lo_ready"], n - 1)
                sp.dma_start(staging(n), (Wq, Wk, Wv, Wo)[n].rearrange("(c p) n -> p c n", p=P)).then_inc(w_loaded[n % 2], 16)

            def next_edges(t):
                sp.wait_ge(s["mask_ready"], t)
                load_edges(0, t)

            for half in range(2):
                sp.dma_start(ring[:, 2 + 4 * half:4 + 4 * half, :].rearrange("p a (c d) -> p (a c) d", d=D),
                             x_t[0, QT // 2 * half:QT // 2 * (half + 1)].rearrange("t p d -> p t d")).then_inc(x_loaded[half], 16)
            load_weights(0)
            load_weights(1)
            for m, bias in enumerate((bq, bk, bv)):
                sp.dma_start(b_in[:, m, :], bias).then_inc(s["const_loaded"], 16)
            sp.dma_start(bo_row[:], bo.partition_broadcast(P)).then_inc(s["const_loaded"], 16)
            sp.dma_start(idt[:], ident).then_inc(s["const_loaded"], 16)
            sp.dma_start(head1[:], headones).then_inc(s["const_loaded"], 16)
            sp.dma_start(ones[:], rowones).then_inc(s["const_loaded"], 16)
            load_edges(0, 0)
            load_weights(2)
            load_weights(3)
            for t in range(1, 5):
                next_edges(t)
            for n, kind in enumerate("qk"):
                sp.wait_ge(s["low_ready"], QT + 2 * n + 2)
                store_parts(kind)
                load_stack(0, 0, kind)
            for t in range(5, QT):
                next_edges(t)

            def graph(b, first, last):
                for up in range(UNITS):
                    U = unit_no(b, up)
                    ending = chunks_ending(up, first, last)
                    for j in range(TILES):
                        kind, t = ending.get(j - 2, NORMS)
                        if kind == "y":
                            sp.wait_ge(s["y_ready"], (b - 1) * QT + t + 1)
                            sp.dma_start(out_t[at(b - 1), t].rearrange("a p d -> p (a d)"), y_out[:, t % 2, :]).then_inc(stored[t % 2], 16)
                            if t < QT - 2:
                                load_x(b - 1, t + 2)
                            elif not last:
                                load_x(b + 1, t + 2 - QT)
                        kind, t = ending.get(j - 3, NORMS)
                        if kind in "qk" and t == 1:
                            sp.wait_ge(s["low_ready"], split_no(b, up, first, last, kind, t) + 1)
                            store_parts(kind)
                        kind, t = ending.get(j - 5, NORMS)
                        if kind in "qk" and t == 1:
                            load_stack(U + 1, (up + 1) % 2, kind)
                        if last:
                            continue
                        if up == 1 and first and j < 2:
                            sp.wait_ge(s["chunk_ready"], QT - 1 + j)
                            load_x(b + 1, j)
                        if up == 2 and j == 0:
                            sp.wait_ge(s["mask_ready"], (b + 1) * QT)
                            load_edges(b + 1, 0)
                        if up == 2 and j % 2 == 0 and 0 < j <= 2 * QT:
                            sp.wait_ge(s["x_stats"], (b + 1) * QT + j // 2)
                            load_x(b + 1, (j // 2 + 1) % QT)
                        kind, t = ending.get(j - 1, NORMS)
                        if kind == "t":
                            sp.wait_ge(s["chunk_ready"], chunk_no(b, up, first, last, "t", t) + 1)
                            load_x(*((b + 1, t + 2) if t < QT - 2 else (b, t + 2 - QT)))
                        if up == UNITS - 1 and j % HG == 0 and j:
                            sp.wait_ge(s["mask_ready"], (b + 1) * QT + j // HG)
                            load_edges(b + 1, j // HG)

            graph(0, True, False)
            with sp.Fori(1, B - 1) as b:
                graph(b, False, False)
            graph(B - 1, False, True)
            for half in range(2):
                sp.wait_ge(s["den_done"], 4 * B * UNITS)
                sp.dma_start(acc[:, 2 * half:2 * half + 2, :].rearrange("p a (c d) -> p (a c) d", d=D),
                             x_t[B - 1, QT // 2 * half:QT // 2 * (half + 1)].rearrange("t p d -> p t d")).then_inc(x_loaded[half], 16)
            for t in range(QT):
                sp.wait_ge(s["y_ready"], (B - 1) * QT + t + 1)
                sp.dma_start(out_t[B - 1, t], x_last(t)).then_inc(stored[t % 2], 16)
            for k in range(2):
                sp.wait_ge(stored[k], 16 * B * QT // 2)

        @block.tensor
        def _(pe):
            def chunk(b, up, first, last, kind, t, hg, piece, of):
                n = chunk_no(b, up, first, last, kind, t)
                splits = split_no(b, up, first, last, kind, t) if kind == "q" else None
                emit_chunk(n, splits, kind, t, hg, b, unit_no(b, up), piece, of)

            def emit_chunk(n, splits, kind, t, hg, b, U, piece=0, of=1, misc=misc, banks=1):
                if piece == 0:
                    chunk_waits(n, splits, kind, t, b, U, banks)
                i = chunk_products(kind, t, hg, piece, of, misc, U)
                if piece == of - 1:
                    i.then_inc(s["chunk_ready"], 1)

            def chunk_waits(n, splits, kind, t, b, U, banks):
                if kind == "q" and t == 0:
                    pe.wait_ge(s["low_ready"], splits)
                if kind == "t":
                    pe.wait_ge(s["x_normed"], (b + 1) * QT + t + 1)
                if kind == "y":
                    pe.wait_ge(s["o_ready"], UNITS * b)
                if kind == "n":
                    pe.wait_ge(s["squared"], 4 * (U + 2))
                if not (isinstance(n, int) and n < banks) and banks < QT:
                    pe.wait_ge(s["chunk_free"], n - banks + 1)

            def chunk_products(kind, t, hg, piece, of, misc, U):
                early = isinstance(U, int) and U < 0
                cols = slice(hg * P, (hg + 1) * P)

                def wanted(index, total):
                    return of * index // total == piece

                if kind == "t":
                    for c in range(DC):
                        tile = x_first(t) if early else x_in[:, t % 2, :]
                        i = nc.tensor.transpose(misc[:, c * P:(c + 1) * P], tile[:, c * P:(c + 1) * P], idt[:])
                elif kind in "qk":
                    which = WQ if kind == "q" else WK
                    terms = [(w, h) for w, h in ((w_hi, hT_hi), (w_hi, hT_lo), (w_lo, hT_hi))]
                    for k, (w, h) in enumerate(terms):
                        for c in range(DC):
                            if not wanted(k * DC + c, 3 * DC):
                                continue
                            i = nc.tensor.matmul(misc, w[which][:, c, cols], h[:, c, t * HALF:(t + 1) * HALF],
                                                 start=k + c == 0, stop=k == 2 and c == DC - 1)
                elif kind == "v":
                    for tt in range(QT // 2):
                        tok = slice((t * QT // 2 + tt) * P, (t * QT // 2 + tt + 1) * P)
                        for k, (w, h) in enumerate(((w_hi, hT_hi), (w_lo, hT_hi), (w_hi, hT_lo))):
                            for c in range(DC):
                                if not wanted((tt * 3 + k) * DC + c, QT // 2 * 3 * DC):
                                    continue
                                i = nc.tensor.matmul(misc[:, tt * P:(tt + 1) * P], h[:, c, tok], w[WV][:, c, cols],
                                                     start=k + c == 0, stop=k == 2 and c == DC - 1)
                elif kind == "n":
                    for j in range(2):
                        for tt in range(QT):
                            i = nc.tensor.matmul(misc[:, (j * QT + tt) * HG:(j * QT + tt + 1) * HG],
                                                 squares[:, j, tt * P:(tt + 1) * P], head1[:], start=True, stop=True)
                elif kind == "y":
                    for k, (w, o) in enumerate(((w_hi, oT_hi), (w_lo, oT_hi), (w_hi, oT_lo))):
                        for c in range(DC):
                            if not wanted(k * DC + c, 3 * DC):
                                continue
                            i = nc.tensor.matmul(misc, o[:, c, t * P:(t + 1) * P], w[WO][:, c, :],
                                                 start=k + c == 0, stop=k == 2 and c == DC - 1)
                return i

            def scores(U, up, j):
                kt, h = divmod(j, HG)
                T = U * TILES + j
                if j == 0:
                    pe.wait_ge(s["stack_loaded"], STACKED * (U + 1))
                if not (isinstance(T, int) and T < 2):
                    pe.wait_ge(s["score_masked"], T - 1)
                for half in range(2):
                    i = nc.tensor.matmul(ps[:, 2 * (j % 2) + half, :], stack["k"][:, up % 2, h, kt * P:(kt + 1) * P],
                                         stack["q"][:, up % 2, h, half * HALF:(half + 1) * HALF], start=True, stop=True)
                i.then_inc(s["score_ready"], 1)

            def pv(U, up, kt, half, very_first):
                if half == 0:
                    pe.wait_ge(s["prob_ready"], U * TILES + HG * (kt + 1))
                if kt == 0 and half == 0 and not very_first:
                    pe.wait_ge(s["o_copied"], 2 * U)
                for h in range(HG):
                    i = nc.tensor.matmul(ps[h * DH:(h + 1) * DH, BANK_O + half, :], v_sb[:, up % 2, kt, h * DH:(h + 1) * DH],
                                         ring[:, slot_of(kt, h), half * HALF:(half + 1) * HALF], start=kt == 0, stop=kt == STEPS - 1,
                                         tile_position=(0, h * DH))
                i.then_inc(s["pv_done"], 1)

            def den(src, half, begin=False, end=False):
                for h in range(HG):
                    i = nc.tensor.matmul(ps[h * DH:(h + 1) * DH, BANK_D, :], ones[:, half, :], src(h, half),
                                         start=begin, stop=end, tile_position=(0, h * DH))
                if half == 1:
                    i.then_inc(s["den_done"], 1)

            def in_ring(kt):
                return lambda h, half: ring[:, slot_of(kt, h), half * HALF:(half + 1) * HALF]

            def in_acc(h, half):
                return acc[:, h, half * HALF:(half + 1) * HALF]

            def tail(U, up, m):
                if m in (0, 2):
                    pv(U, up, STEPS - 1, m // 2, False)
                if m in (1, 2):
                    den(in_ring(STEPS - 1), m - 1)
                if m == 3:
                    pe.wait_ge(s["sum_done"], 16 * U + 16)
                if m in (3, 4):
                    den(in_acc, m - 3, end=m == 4)

            def graph(b, first, last):
                for up in range(UNITS):
                    U = unit_no(b, up)
                    ending = chunks_ending(up, first, last)
                    for j in range(TILES):
                        kt, h = divmod(j, HG)
                        if j + 1 < TILES:
                            scores(U, up, j + 1)
                        elif not (last and up == UNITS - 1):
                            scores(U + 1, up + 1, 0)
                        if j <= HG and not (first and up == 0):
                            tail(U - 1, (up + 1) % 2, j)
                        if kt and h % 2 == 0:
                            pv(U, up, kt - 1, h // 2, first and up == 0)
                        if kt == 4 and h == 1:
                            if not (first and up == 0):
                                pe.wait_ge(s["ln_done"], U)
                            pe.wait_ge(s["sum_done"], 16 * U + 8)
                        if kt == 4 and h % 2:
                            den(in_acc, h // 2, begin=h == 1)
                        if kt == 7 and h % 2:
                            den(in_ring(STEPS - 2), h // 2)
                        for at_, of, kind, t in chunk_plan(up, first, last):
                            if at_ <= j < at_ + of:
                                chunk(b, up, first, last, kind, t, (up + 1) % UNITS, j - at_, of)

            pe.wait_ge(s["const_loaded"], 16 * 7)
            for n, (kind, t) in enumerate(PRO_CHUNKS):
                if (kind, t) in PROJ[::2]:
                    pe.wait_ge(s["w_lo_ready"], "qkv".index(kind) + 1)
                emit_chunk(n, count(SPLIT, PRO_CHUNKS[:n]), kind, t, 0, -1, -1, misc=early_bank(n), banks=EARLY_BANKS)
            pe.wait_ge(s["w_lo_ready"], 4)
            pe.wait_ge(s["chunk_free"], len(PRO_CHUNKS))
            scores(0, 0, 0)
            graph(0, True, False)
            with pe.Fori(1, B - 1) as b:
                graph(b, False, False)
            graph(B - 1, False, True)
            U = B * UNITS - 1
            for m in range(HG + 1):
                tail(U, 1, m)
            base = last_base()
            for t in range(QT):
                emit_chunk(base + t, None, "y", t, 0, B, None, misc=ps[:, t, :], banks=QT)

        @block.scalar
        def _(act):
            def exp(U, j):
                act.wait_ge(s["score_masked"], U * TILES + j + 1)
                r = ring[:, slot_of(*divmod(j, HG)), :]
                nc.scalar.activation(r, r, ACT.Exp, scale=SCALE / UP / UP).then_inc(s["prob_ready"], 1)

            def chunk(n, ns, kind, t, up, hg, parity, restacked, spare, misc=misc):
                act.wait_ge(s["chunk_ready"], n + 1)
                half = slice(t * HALF, (t + 1) * HALF)
                if kind in "qkt":
                    if not (isinstance(ns, int) and ns < 2):
                        act.wait_ge(s["low_ready"], ns - 1)
                    if kind == "t":
                        nc.scalar.activation(full[:, parity, :], misc, ACT.Relu).then_inc(s["chunk_free"], 1)
                    else:
                        j = "qk".index(kind)
                        nc.scalar.activation(full[:, parity, :], misc, ACT.Identity, bias=b_up[:, j, hg:hg + 1]).then_inc(s["chunk_free"], 1)
                    act.wait_ge(s["chunk_free"], n + 1)
                    if restacked is not None:
                        act.wait_ge(s[kind + "_stored"], restacked)
                    if kind == "t":
                        high = hT_hi[:, :, t * P:(t + 1) * P]
                        nc.scalar.activation(high, full[:, parity, :].rearrange("p (c n) -> p c n", n=P), ACT.Copy).then_inc(s["high_ready"], 1)
                    else:
                        nc.scalar.activation(part[kind][:, 0, half], full[:, parity, :], ACT.Copy).then_inc(s["high_ready"], 1)
                elif kind == "v":
                    if spare is not None:
                        act.wait_ge(s["pv_done"], spare)
                    nc.scalar.activation(v_sb[:, (up + 1) % 2, t * QT // 2:(t + 1) * QT // 2, :],
                                         misc.rearrange("p (c n) -> p c n", n=P), ACT.Copy).then_inc(s["chunk_free"], 1)

            def square(ns, kind, t, normed):
                half = slice(t * HALF, (t + 1) * HALF)
                act.wait_ge(s["high_ready"], ns + 1)
                if normed is not None:
                    act.wait_ge(s["chunk_ready"], normed)
                nc.scalar.activation(squares[:, "qk".index(kind), half], part[kind][:, 0, half], ACT.Square, scale=1 / UP).then_inc(s["squared"], 1)

            def copy_o(U, half):
                if half == 0 and not (isinstance(U, int) and U == 0):
                    act.wait_ge(s["o_ready"], U)
                act.wait_ge(s["pv_done"], 16 * U + 15 + half)
                nc.scalar.activation(o_raw[:, half * HALF:(half + 1) * HALF], ps[:, BANK_O + half, :], ACT.Copy).then_inc(s["o_copied"], 1)

            def reciprocal(U):
                act.wait_ge(s["den_done"], 4 * U + 4)
                nc.scalar.activation(rden, ps[:, BANK_D, :], ACT.Ln).then_inc(s["ln_done"], 1)
                act.wait_ge(s["ln_done"], U + 1)
                nc.scalar.activation(rden, rden, ACT.Exp, scale=-1.0).then_inc(s["rden_ready"], 1)

            def o_high(U, c, y_read):
                act.wait_ge(s["o_scaled"], U + 1)
                if y_read is not None:
                    act.wait_ge(s["chunk_ready"], y_read)
                nc.scalar.activation(oT_hi[:, c, :], o_raw[:], ACT.Identity, bias=b_up[:, 2, c:c + 1]).then_inc(s["o_hi_ready"], 1)

            def rstds(g):
                act.wait_ge(s["x_mean"], g + 1)
                nc.scalar.activation(rstd[:], mv[:, :, 1], ACT.Ln, bias=eps[:]).then_inc(s["ln_var"], 1)
                act.wait_ge(s["ln_var"], g + 1)
                nc.scalar.activation(rstd[:], rstd[:], ACT.Exp, scale=-0.5).then_inc(s["rstd_ready"], 1)

            def graph(b, first, last):
                for up in range(UNITS):
                    U = unit_no(b, up)
                    ending = chunks_ending(up, first, last)
                    for j in range(TILES):
                        exp(U, j)
                        if not (first and up == 0):
                            if j in (1, 3):
                                copy_o(U - 1, j // 2)
                            if j == 5:
                                reciprocal(U - 1)
                            if j == o_high_at(up, first):
                                y_read = None
                                if up == 1 and not first:
                                    y_read = chunk_no(b, 1, first, last, "y", QT - 1) + 1
                                o_high(U - 1, (up - 1) % UNITS, y_read)
                        if up == 2 and j == 24 and not last:
                            rstds(b + 1)
                        if j in ending:
                            kind, t = ending[j]
                            if kind in "qkvt":
                                restacked = spare = None
                                if kind in "qk":
                                    restacked = 16 * (U + 1)
                                if kind == "v" and not (first and up == 0):
                                    spare = 16 * U
                                ns = split_no(b, up, first, last, kind, t) if kind in SPLIT else None
                                chunk(chunk_no(b, up, first, last, kind, t), ns, kind, t, up, (up + 1) % UNITS,
                                      split_parity(up, first, last, kind, t), restacked, spare)
                        if j in SQUARES_AT and ending:
                            kind, t = SQUARES_AT[j]
                            square(split_no(b, up, first, last, kind, t), kind, t,
                                   chunk_no(b, up, first, last, "q", 0))

            nc.scalar.preload_act_table_set("natural_log_exp_and_others")
            def weights_high(n):
                act.wait_ge(w_loaded[n % 2], 16 * (n // 2 + 1))
                nc.scalar.activation(w_hi[n][:], staging(n), ACT.Copy, scale=UP).then_inc(s["w_hi_ready"], 1)

            weights_high(0)
            weights_high(1)
            act.wait_ge(s["const_ready"], 4)
            rstds(0)
            for n, (kind, t) in enumerate(PRO_CHUNKS):
                if kind in "qkvt":
                    ns = count(SPLIT, PRO_CHUNKS[:n])
                    chunk(n, ns, kind, t, -1, 0, ns % 2, None, None, misc=early_bank(n))
                if (kind, t) in WEIGHTS_AFTER:
                    weights_high(WEIGHTS_AFTER[kind, t])
                if kind in "qk":
                    square(count(SPLIT, PRO_CHUNKS[:n]), kind, t, None)
            graph(0, True, False)
            with act.Fori(1, B - 1) as b:
                graph(b, False, False)
            graph(B - 1, False, True)
            U = B * UNITS - 1
            for half in range(2):
                copy_o(U, half)
            reciprocal(U)
            o_high(U, UNITS - 1, None)

        @block.vector
        def _(dve):
            def masked(U, j, very_first):
                kt, h = divmod(j, HG)
                if not (very_first and kt < 2):
                    if h == 0:
                        dve.wait_ge(s["pv_done"], 16 * U + 2 * kt - 2)
                    if kt < 2:
                        if h == 0:
                            dve.wait_ge(s["den_done"], 4 * U + kt - 2)
                    else:
                        dve.wait_ge(s["sum_done"], 16 * U + {2: 0, 3: 0, 4: 4, 5: 8, 6: 8, 7: 12}[kt] + h + 1)
                dve.wait_ge(s["score_ready"], U * TILES + j + 1)
                nc.vector.tensor_tensor(ring[:, slot_of(kt, h), :], ps_s(j), mask[:, kt, :], ALU.add).then_inc(s["score_masked"], 1)

            def chunk(n, nsplit, kind, t, g, parity, misc=misc):
                half = slice(t * HALF, (t + 1) * HALF)
                if kind in "qkt":
                    dve.wait_ge(s["high_ready"], nsplit + 1)
                else:
                    dve.wait_ge(s["chunk_ready"], n + 1)
                if kind == "t":
                    nc.vector.tensor_tensor(hT_lo[:, :, t * P:(t + 1) * P], full[:, parity, :].rearrange("p (c n) -> p c n", n=P),
                                            hT_hi[:, :, t * P:(t + 1) * P], ALU.subtract).then_inc(s["low_ready"], 1)
                elif kind in "qk":
                    nc.vector.tensor_tensor(part[kind][:, 1, half], full[:, parity, :], part[kind][:, 0, half], ALU.subtract)\
                        .then_inc(s["low_ready"], 1)
                elif kind == "n":
                    nc.vector.tensor_tensor(norms[:], misc[:, 0:2 * QT * HG], norms[:], ALU.max).then_inc(s["chunk_free"], 1)
                elif kind == "y":
                    dve.wait_ge(s["x_biased"], g * QT + t + 1)
                    if not (isinstance(g, int) and g == 0 and t < 2):
                        dve.wait_ge(stored[t % 2], 16 * (g * (QT // 2) + t // 2))
                    nc.vector.scalar_tensor_tensor(out=y_out[:, t % 2, :], in0=misc, scalar=1 / UP / UP, in1=x_in[:, t % 2, :],
                                                   op0=ALU.mult, op1=ALU.add).then_inc(s["y_ready"], 1)
                    dve.wait_ge(s["y_ready"], g * QT + t + 1)
                    nc.vector.memset(gap[:], 0.0).then_inc(s["chunk_free"], 1)

            def statistic(b, first, g, t):
                if b is None:
                    dve.wait_ge(x_loaded[t // (QT // 2)], 16)
                else:
                    x_landed(dve, b, first, "s", t)
                tile = x_first(t) if b is None else x_in[:, t % 2, :]
                nc.vector.bn_stats(stats[:, t, :], tile).then_inc(s["x_stats"], 1)

            def means(g):
                dve.wait_ge(s["x_stats"], (g + 1) * QT)
                nc.vector.memset(gap[:], 0.0)
                for t in range(QT):
                    i = nc.vector.bn_aggr(mv[:, t, :], stats[:, t, :])
                i.then_inc(s["x_mean"], 1)

            def normalise(b, first, g, t):
                if b is not None:
                    x_landed(dve, b, first, "n", t)
                if t == 0:
                    dve.wait_ge(s["rstd_ready"], g + 1)
                tile = x_first(t) if b is None else x_in[:, t % 2, :]
                nc.vector.tensor_scalar(tile, tile, mv[:, t, 0:1], rstd[:, t:t + 1],
                                        ALU.subtract, ALU.mult).then_inc(s["x_normed"], 1)

            def to_mask(g, kt):
                dve.wait_ge(s["edges_loaded"], 16 * (g * QT + kt + 1))
                nc.vector.tensor_scalar(mask[:, kt, :], edges[:], 0.0, MASKED, ALU.is_equal, ALU.mult).then_inc(s["mask_ready"], 1)

            def spread(U):
                dve.wait_ge(s["rden_ready"], U + 1)
                nc.vector.memset(gap[:], 0.0)
                for half in range(2):
                    nc.vector.stream_shuffle(rden_all[:, half * HALF:(half + 1) * HALF], rden, [half] * 32).then_inc(s["shuffled"], 1)

            def scale_o(U):
                dve.wait_ge(s["shuffled"], 2 * U + 2)
                dve.wait_ge(s["o_copied"], 2 * U + 2)
                nc.vector.tensor_tensor(o_raw[:], o_raw[:], rden_all[:], ALU.mult).then_inc(s["o_scaled"], 1)

            def o_low(U, c):
                dve.wait_ge(s["o_hi_ready"], U + 1)
                nc.vector.scalar_tensor_tensor(out=oT_lo[:, c, :], in0=o_raw[:], scalar=b_up[:, 2, c:c + 1], in1=oT_hi[:, c, :],
                                               op0=ALU.add, op1=ALU.subtract).then_inc(s["o_ready"], 1)

            def graph(b, first, last):
                for up in range(UNITS):
                    U = unit_no(b, up)
                    ending = chunks_ending(up, first, last)
                    for j in range(TILES):
                        kt, h = divmod(j, HG)
                        if up == 0 and j == 0:
                            dve.wait_ge(s["mask_ready"], QT - 2 if first else (b + 1) * QT)
                        if first and up == 0 and kt >= QT - 2 and h == 0:
                            dve.wait_ge(s["mask_ready"], kt + 1)
                        masked(U, j, first and up == 0)
                        if not (first and up == 0):
                            if j == 7:
                                spread(U - 1)
                            if j == 8:
                                scale_o(U - 1)
                            if j == o_high_at(up, first) + 1:
                                o_low(U - 1, (up - 1) % UNITS)
                        if first and up == 0 and j in (7, 11):
                            to_mask(0, QT - 2 + j // 11)
                        if first and up == 0 and j in (12, 14, 16, 18):
                            n = (j - 12) // 2
                            nc.vector.tensor_reduce(limits[:, LIM_W + n:LIM_W + n + 1], w_hi[n][:], AX.XY, ALU.max, apply_absolute_value=True)\
                                .then_inc(s["limits_ready"], 1)
                        if first and up == 0 and j == 20:
                            nc.vector.tensor_reduce(limits[:, LIM_B:LIM_B + 1], b_up[:, 2, :], AX.X, ALU.max, apply_absolute_value=True)\
                                .then_inc(s["limits_ready"], 1)
                        if up == 2 and not last:
                            if j % 2 == 1 and j < 2 * QT:
                                statistic(b, first, b + 1, j // 2)
                            if j == 21:
                                means(b + 1)
                        if up == UNITS - 1 and not last:
                            for at_, _, kind, t in chunk_plan(up, first, last):
                                if kind == "t" and at_ - 1 == j:
                                    normalise(b, first, b + 1, t)
                            if h == HG - 1:
                                dve.wait_ge(s["score_masked"], U * TILES + j + 1)
                                to_mask(b + 1, kt)
                        for kind, t in [c for c in (ending.get(j - 2),) if c and c[0] in SPLIT] + \
                                       [c for c in (ending.get(j - 1),) if c and c[0] in "ny"]:
                            n = chunk_no(b, up, first, last, kind, t)
                            ns = split_no(b, up, first, last, kind, t) if kind in SPLIT else None
                            chunk(n, ns, kind, t, b - 1 if kind == "y" else None, split_parity(up, first, last, kind, t))

            nc.vector.memset(eps[:], EPS).then_inc(s["const_ready"], 1)
            nc.vector.memset(norms[:], 0.0).then_inc(s["const_ready"], 1)
            def weights_low(n):
                dve.wait_ge(s["w_hi_ready"], n + 1)
                nc.vector.scalar_tensor_tensor(out=w_lo[n][:], in0=staging(n), scalar=UP, in1=w_hi[n][:], op0=ALU.mult, op1=ALU.subtract)\
                    .then_inc(s["w_lo_ready"], 1)

            for t in range(QT):
                statistic(None, True, 0, t)
            dve.wait_ge(s["const_loaded"], 16 * 7)
            nc.vector.tensor_scalar(b_up[:], b_in[:], UP, None, ALU.mult).then_inc(s["const_ready"], 1)
            nc.vector.memset(gap[:], 0.0).then_inc(s["const_ready"], 1)
            dve.wait_ge(s["const_ready"], 4)
            means(0)
            weights_low(0)
            for t in range(QT):
                normalise(None, True, 0, t)
            weights_low(1)
            to_mask(0, 0)
            for n, (kind, t) in enumerate(PRO_CHUNKS):
                if kind != "v":
                    ns = count(SPLIT, PRO_CHUNKS[:n])
                    chunk(n, ns, kind, t, None, ns % 2, misc=early_bank(n))
                if (kind, t) in WEIGHTS_AFTER:
                    weights_low(WEIGHTS_AFTER[kind, t])
                if kind == "t" and t % 2:
                    to_mask(0, (t + 1) // 2)
            to_mask(0, 5)
            graph(0, True, False)
            with dve.Fori(1, B - 1) as b:
                graph(b, False, False)
            graph(B - 1, False, True)
            U = B * UNITS - 1
            spread(U)
            scale_o(U)
            o_low(U, UNITS - 1)
            base = last_base()
            for t in range(QT):
                dve.wait_ge(s["chunk_ready"], base + t + 1)
                dve.wait_ge(s["x_biased"], (B - 1) * QT + t + 1)
                nc.vector.scalar_tensor_tensor(out=x_last(t), in0=ps[:, t, :], scalar=1 / UP / UP, in1=x_last(t),
                                               op0=ALU.mult, op1=ALU.add).then_inc(s["y_ready"], 1)
            nc.vector.tensor_reduce(limits[:, LIM_N:LIM_QK].rearrange("p (j h) -> p j h", j=2), norms[:].rearrange("p (j t h) -> p j h t", j=2, t=QT),
                                    AX.X, ALU.max).then_inc(s["limits_ready"], 1)
            dve.wait_ge(s["limits_everywhere"], 1)
            nc.vector.scalar_tensor_tensor(out=limits[:, LIM_QK:LIMITS], in0=limits[:, LIM_N:LIM_N + HG], scalar=SCALE * SCALE,
                                           in1=limits[:, LIM_N + HG:LIM_QK], op0=ALU.mult, op1=ALU.mult).then_inc(s["verdict_step"], 1)
            nc.vector.tensor_scalar(limits[:, LIM_W:LIM_W + 4], limits[:, LIM_W:LIM_W + 4], BOUND_SQ / (W_MAX * UP), None, ALU.mult)\
                .then_inc(s["verdict_step"], 1)
            dve.wait_ge(s["verdict_step"], 2)
            nc.vector.reduce_max(largest[:], limits[:], AX.X).then_inc(s["verdict_step"], 1)
            dve.wait_ge(s["verdict_step"], 3)
            nc.vector.tensor_scalar(flag[:], largest[0:1, :], BOUND_SQ, None, ALU.is_gt).then_inc(s["verdict_step"], 1)

        @block.gpsimd
        def _(pool):
            def sums(U, kt, h, very_first):
                group, k = divmod(kt, 3)
                pool.wait_ge(s["prob_ready"], U * TILES + HG * kt + h + 1)
                if k == 1 and h == 0:
                    if group == 1:
                        pool.wait_ge(s["den_done"], 4 * U + 1)
                    elif not very_first:
                        pool.wait_ge(s["den_done"], 4 * U)
                first = ring[:, slot_of(kt - 1, h), :] if k == 1 else acc[:, h, :]
                nc.gpsimd.tensor_tensor(acc[:, h, :], first, ring[:, slot_of(kt, h), :], ALU.add).then_inc(s["sum_done"], 1)

            def bias_x(b, first, g, t):
                if b is None:
                    pool.wait_ge(x_loaded[t // (QT // 2)], 16 * (B * (3 * QT // 2) + 1 - 3 * (QT // 2) + 1))
                else:
                    x_landed(pool, b, first, "y", t)
                tile = x_last(t) if b is None else x_in[:, t % 2, :]
                nc.gpsimd.tensor_tensor(tile, tile, bo_row[:], ALU.add).then_inc(s["x_biased"], 1)

            def graph(b, first, last):
                for up in range(UNITS):
                    U = unit_no(b, up)
                    for j in range(TILES):
                        kt, h = divmod(j, HG)
                        if not first and up < 2:
                            for t in range(QT):
                                if up * TILES + j == (OUTPUT_AT[t - 2] + 4 if t >= 2 else 2 + t):
                                    bias_x(b, first, b - 1, t)
                        if kt in (1, 2, 4, 5):
                            sums(U, kt, h, first and up == 0)

            pool.wait_ge(s["const_loaded"], 16 * 7)
            graph(0, True, False)
            with pool.Fori(1, B - 1) as b:
                graph(b, False, False)
            graph(B - 1, False, True)
            for t in range(QT):
                bias_x(None, False, B - 1, t)
            pool.wait_ge(s["limits_ready"], 6)
            nc.gpsimd.partition_all_reduce(limits[:, 0:LIM_QK], limits[:, 0:LIM_QK], P, RMAX).then_inc(s["limits_everywhere"], 1)


def program(nc, x, adj, adjT, Wq, bq, Wk, bk, Wv, bv, bv_cols, Wo, bo, ident, headones, rowones, out):
    scratch = [nc.dram_tensor(n, shape, F32, kind="Internal").ap()
               for n, shape in (("qT_s", [B, D, S]), ("kT_s", [B, D, S]), ("v_s", [B, S, D]), ("o_s", [B, S, D]))]
    parts = {c: nc.dram_tensor(c + "_parts", [P, 2, S], F16, kind="Internal").ap() for c in "qk"}
    with nc.sbuf_tensor("flag", [1, 1], I32) as flag:
        fast_attention(nc, x, adjT, Wq, bq, Wk, bk, Wv, bv_cols, Wo, bo, ident, headones, rowones, out, parts, flag)
        general_attention(nc, flag[0:1, 0:1], x, adj, Wq, bq, Wk, bk, Wv, bv, Wo, bo, ident, out, scratch)


def kernel(x, adj, L0_gnn_Wq, L0_gnn_bq, L0_gnn_Wk, L0_gnn_bk, L0_gnn_Wv, L0_gnn_bv, L0_gnn_Wo, L0_gnn_bo):
    import numpy as np
    import concourse.bacc as bacc
    from concourse.bass_utils import run_bass_kernel_spmd

    nc = bacc.Bacc("TRN2", target_bir_lowering=False, num_devices=1)
    heads = np.arange(P)[:, None] // DH == np.arange(HG)
    rows = np.broadcast_to(np.arange(DH) % 2 == np.arange(2)[:, None], (P, 2, DH))
    arrays = {
        "x": x, "adj": adj, "adjT": np.swapaxes(np.asarray(adj), 1, 2),
        "Wq": L0_gnn_Wq, "bq": np.asarray(L0_gnn_bq).reshape(DC, P).T, "Wk": L0_gnn_Wk, "bk": np.asarray(L0_gnn_bk).reshape(DC, P).T,
        "Wv": L0_gnn_Wv, "bv": L0_gnn_bv, "bv_cols": np.asarray(L0_gnn_bv).reshape(DC, P).T, "Wo": L0_gnn_Wo, "bo": L0_gnn_bo,
        "ident": np.eye(P, dtype=np.float32), "headones": heads.astype(mybir.dt.np(BF16)), "rowones": rows.astype(np.float32),
    }
    arrays = {n: np.ascontiguousarray(a) for n, a in arrays.items()}
    args = [nc.dram_tensor(n, a.shape, mybir.dt.from_np(a.dtype), kind="ExternalInput").ap() for n, a in arrays.items()]
    out = nc.dram_tensor("out", (B, S, D), F32, kind="ExternalOutput").ap()
    program(nc, *args, out)
    r = run_bass_kernel_spmd(nc, [arrays], core_ids=[0])
    return r.results[0]["out"]
```
